# Optimizing a Trainium2 kernel written in Bass

```python
import numpy as np
import jax
import jax.numpy as jnp

def _softmax(x, axis=-1):
    return jax.nn.softmax(x, axis=axis)

def _gelu(x):
    return jax.nn.gelu(x, approximate=True)

def _silu(x):
    return jax.nn.silu(x)

def _sigmoid(x):
    return jax.nn.sigmoid(x)

def _layernorm(x, axis=-1, eps=1e-05):
    m = jnp.mean(x, axis=axis, keepdims=True)
    v = jnp.var(x, axis=axis, keepdims=True)
    return (x - m) / jnp.sqrt(v + eps)

def _scatter_add(tgt, idx, src, axis=0):
    return tgt.at[idx].add(src)

def _segment_sum(src, seg, n):
    return jax.ops.segment_sum(src, seg, n)
kernel_name = 'mk_flamingo_gated_d2_seqx_r4_1404dd'

def setup_inputs(seed: int=0):
    np.random.seed(seed)
    _w = jnp.asarray

    def _rec_inputs():
        import jax
        import jax.numpy as jnp
        _rk = jax.random.key(seed)
        x = 0.0003765 + 1 * jax.random.normal(jax.random.fold_in(_rk, 1), (64, 256, 256), jnp.float32)
        _lenS = 256 - jax.random.randint(jax.random.fold_in(_rk, 7), (64,), 0, max(1, 256 // 4) + 1, jnp.int32)
        _lenS2 = 120 - jax.random.randint(jax.random.fold_in(_rk, 8), (64,), 0, max(1, 120 // 4) + 1, jnp.int32)
        _ctx_1024P = jax.random.normal(jax.random.fold_in(_rk, 11), (64, 16, 256), jnp.float32)
        _ctx_1024c = jax.random.dirichlet(jax.random.fold_in(_rk, 511), 0.3 * jnp.ones((16,), jnp.float32), (64, 120))
        _ctx_1024t = jnp.einsum('bsk,bkd->bsd', _ctx_1024c, _ctx_1024P)
        _ctx_1024t = _ctx_1024t * jax.lax.rsqrt(jnp.mean(jnp.square(_ctx_1024t)) + 1e-12) * 0.953939
        ctx_1024 = -0.000292821 + 1.00034 * (_ctx_1024t + 0.3 * jax.random.normal(jax.random.fold_in(_rk, 611), (64, 120, 256), jnp.float32))
        _g = jax.random.normal(jax.random.fold_in(_rk, 9001), (2, 2), jnp.float32)
        _g = jnp.sign(_g) * jnp.maximum(jnp.abs(_g), 1.0) + (_g == 0) * 1.0
        g_xattn = _g[0]
        g_ffn = _g[1]
        return (x, ctx_1024, g_xattn, g_ffn)
    x, ctx_1024, g_xattn, g_ffn = _rec_inputs()

    def _L0_xattn_setup():
        import jax, jax.numpy as jnp
        import numpy as np
        NUM_HEADS = 16

        def _split_heads(x, num_heads):
            B, S, H = x.shape
            dh = H // num_heads
            return x.reshape(B, S, dh, num_heads).transpose(0, 3, 1, 2)
        key = jax.random.key(seed)
        ks = jax.random.split(key, 11)
        B, S, D, H = (2, 512, 256, 256)
        s = lambda k, shape, scale=1.0: jax.random.normal(k, shape, dtype=jnp.float32) * scale
        return {'KEY': s(ks[0], (B, S, D)), 'VALUE': s(ks[1], (B, S, D)), 'QUERY': s(ks[2], (B, S, D)), 'Wk_w': s(ks[3], (H, D), 0.02), 'Wk_b': s(ks[4], (H,), 0.02), 'Wq_w': s(ks[5], (H, D), 0.02), 'Wq_b': s(ks[6], (H,), 0.02), 'Wv_w': s(ks[7], (H, D), 0.02), 'Wv_b': s(ks[8], (H,), 0.02), 'Wo_w': s(ks[9], (H, H), 0.02), 'Wo_b': s(ks[10], (H,), 0.02)}
    _L0_xattn_all = _L0_xattn_setup()
    _L0_xattn_in = {k: v for k, v in _L0_xattn_all.items() if k in ('Wk_w', 'Wk_b', 'Wq_w', 'Wq_b', 'Wv_w', 'Wv_b', 'Wo_w', 'Wo_b')}
    del _L0_xattn_all

    def _L0_ffn_setup():
        import jax, jax.numpy as jnp
        import numpy as np
        DIM = 256
        HIDDEN = 768
        SCALE = 1.0 / 127.0

        def _dequant(w_int, dtype):
            return w_int.astype(dtype) * jnp.asarray(SCALE, dtype)
        key = jax.random.key(seed)
        k_x, k_g, k_u, k_d = jax.random.split(key, 4)
        x = jax.random.normal(k_x, (4, 512, DIM), dtype=jnp.float32)
        w_gate = jax.random.randint(k_g, (HIDDEN, DIM), -127, 128, dtype=jnp.int32)
        w_up = jax.random.randint(k_u, (HIDDEN, DIM), -127, 128, dtype=jnp.int32)
        w_down = jax.random.randint(k_d, (DIM, HIDDEN), -127, 128, dtype=jnp.int32)
        return {'x': x, 'w_gate': w_gate, 'w_up': w_up, 'w_down': w_down}
    _L0_ffn_all = _L0_ffn_setup()
    _L0_ffn_in = {k: v for k, v in _L0_ffn_all.items() if k in ('w_gate', 'w_up', 'w_down')}
    del _L0_ffn_all

    def _L1_xattn_setup():
        import jax, jax.numpy as jnp
        import numpy as np
        B, N, T, D, H = (2, 512, 512, 256, 16)
        HD = D // H
        key = jax.random.key(seed)
        ks = jax.random.split(key, 5)
        s = 0.02
        return {'x': jax.random.normal(ks[0], (B, N, D), dtype=jnp.float32), 'context': jax.random.normal(ks[1], (B, T, D), dtype=jnp.float32), 'Wq': jax.random.normal(ks[2], (D, D), dtype=jnp.float32) * s, 'Wkv': jax.random.normal(ks[3], (D, 2 * HD), dtype=jnp.float32) * s, 'Wo': jax.random.normal(ks[4], (D, D), dtype=jnp.float32) * s}
    _L1_xattn_all = _L1_xattn_setup()
    _L1_xattn_in = {k: v for k, v in _L1_xattn_all.items() if k in ('Wq', 'Wkv', 'Wo')}
    del _L1_xattn_all

    def _L1_ffn_setup():
        import jax, jax.numpy as jnp
        import numpy as np
        ALPHA = 1.0
        key = jax.random.key(seed)
        ks = jax.random.split(key, 7)
        B, S, IN, OUT = (8, 2048, 256, 256)
        RANK, DDIM, UDIM = (4, 100, 50)
        return {'hidden_states': jax.random.normal(ks[0], (B, S, IN), dtype=jnp.float32), 'W': jax.random.normal(ks[1], (OUT, IN), dtype=jnp.float32) * 0.02, 'b': jax.random.normal(ks[2], (OUT,), dtype=jnp.float32) * 0.02, 'lora_down': jax.random.normal(ks[3], (RANK, DDIM), dtype=jnp.float32) * 0.1, 'lora_up': jax.random.normal(ks[4], (UDIM, RANK), dtype=jnp.float32) * 0.1, 'down_aux': jax.random.normal(ks[5], (DDIM, IN), dtype=jnp.float32) * 0.03, 'up_aux': jax.random.normal(ks[6], (OUT, UDIM), dtype=jnp.float32) * 0.03}
    _L1_ffn_all = _L1_ffn_setup()
    _L1_ffn_in = {k: v for k, v in _L1_ffn_all.items() if k in ('W', 'b', 'lora_down', 'lora_up', 'down_aux', 'up_aux')}
    del _L1_ffn_all
    return {'x': x, 'ctx_1024': ctx_1024, 'g_xattn': g_xattn, 'g_ffn': g_ffn, 'L0_xattn_Wk_w': _L0_xattn_in['Wk_w'], 'L0_xattn_Wk_b': _L0_xattn_in['Wk_b'], 'L0_xattn_Wq_w': _L0_xattn_in['Wq_w'], 'L0_xattn_Wq_b': _L0_xattn_in['Wq_b'], 'L0_xattn_Wv_w': _L0_xattn_in['Wv_w'], 'L0_xattn_Wv_b': _L0_xattn_in['Wv_b'], 'L0_xattn_Wo_w': _L0_xattn_in['Wo_w'], 'L0_xattn_Wo_b': _L0_xattn_in['Wo_b'], 'L0_ffn_w_gate': _L0_ffn_in['w_gate'], 'L0_ffn_w_up': _L0_ffn_in['w_up'], 'L0_ffn_w_down': _L0_ffn_in['w_down'], 'L1_xattn_Wq': _L1_xattn_in['Wq'], 'L1_xattn_Wkv': _L1_xattn_in['Wkv'], 'L1_xattn_Wo': _L1_xattn_in['Wo'], 'L1_ffn_W': _L1_ffn_in['W'], 'L1_ffn_b': _L1_ffn_in['b'], 'L1_ffn_lora_down': _L1_ffn_in['lora_down'], 'L1_ffn_lora_up': _L1_ffn_in['lora_up'], 'L1_ffn_down_aux': _L1_ffn_in['down_aux'], 'L1_ffn_up_aux': _L1_ffn_in['up_aux']}

def reference(x, ctx_1024, g_xattn, g_ffn, L0_xattn_Wk_w, L0_xattn_Wk_b, L0_xattn_Wq_w, L0_xattn_Wq_b, L0_xattn_Wv_w, L0_xattn_Wv_b, L0_xattn_Wo_w, L0_xattn_Wo_b, L0_ffn_w_gate, L0_ffn_w_up, L0_ffn_w_down, L1_xattn_Wq, L1_xattn_Wkv, L1_xattn_Wo, L1_ffn_W, L1_ffn_b, L1_ffn_lora_down, L1_ffn_lora_up, L1_ffn_down_aux, L1_ffn_up_aux):
    import jax
    import jax.numpy as jnp

    def _L0_xattn_ref(KEY, VALUE, QUERY, Wk_w, Wk_b, Wq_w, Wq_b, Wv_w, Wv_b, Wo_w, Wo_b):
        import jax, jax.numpy as jnp
        import numpy as np
        NUM_HEADS = 16

        def _split_heads(x, num_heads):
            B, S, H = x.shape
            dh = H // num_heads
            return x.reshape(B, S, dh, num_heads).transpose(0, 3, 1, 2)
        nh = NUM_HEADS
        k = _split_heads(KEY @ Wk_w.T + Wk_b, nh)
        q = _split_heads(QUERY @ Wq_w.T + Wq_b, nh)
        v = _split_heads(VALUE @ Wv_w.T + Wv_b, nh)
        dh = q.shape[-1]
        score = jnp.einsum('bhij,bhkj->bhik', k, q) / jnp.sqrt(jnp.asarray(dh, k.dtype))
        attn = jax.nn.softmax(score, axis=1)
        out = jnp.einsum('bhik,bhij->bhjk', attn, v)
        B = out.shape[0]
        out = out.transpose(0, 2, 1, 3).reshape(B, -1, out.shape[-1]).transpose(0, 2, 1)
        res = out @ Wo_w.T + Wo_b
        return res

    def _L0_ffn_ref(x, w_gate, w_up, w_down):
        import jax, jax.numpy as jnp
        import numpy as np
        DIM = 256
        HIDDEN = 768
        SCALE = 1.0 / 127.0

        def _dequant(w_int, dtype):
            return w_int.astype(dtype) * jnp.asarray(SCALE, dtype)
        wg = _dequant(w_gate, x.dtype)
        wu = _dequant(w_up, x.dtype)
        wd = _dequant(w_down, x.dtype)
        gate = jnp.einsum('bsd,hd->bsh', x, wg)
        up = jnp.einsum('bsd,hd->bsh', x, wu)
        h = jax.nn.silu(gate) * up
        return jnp.einsum('bsh,dh->bsd', h, wd)

    def _L1_xattn_ref(x, context, Wq, Wkv, Wo):
        import jax, jax.numpy as jnp
        import numpy as np
        B, N, T, D, H = (2, 512, 512, 256, 16)
        HD = D // H
        b, n, d = x.shape
        h = H
        hd = d // h
        scale = hd ** (-0.5)
        q = x @ Wq
        kv = context @ Wkv
        k, v = jnp.split(kv, 2, axis=-1)
        q = q.reshape(b, n, h, hd).transpose(0, 2, 1, 3) * scale
        sim = jnp.einsum('bhnd,btd->bhnt', q, k)
        att = jax.nn.softmax(sim, axis=-1)
        y = jnp.einsum('bhnt,btd->bhnd', att, v)
        y = y.transpose(0, 2, 1, 3).reshape(b, n, d)
        return y @ Wo

    def _L1_ffn_ref(hidden_states, W, b, lora_down, lora_up, down_aux, up_aux):
        import jax, jax.numpy as jnp
        import numpy as np
        ALPHA = 1.0
        lilora_weight = up_aux @ (lora_up @ (lora_down @ down_aux))
        base = jnp.einsum('bsi,oi->bso', hidden_states, W) + b
        delta = jnp.einsum('bsi,oi->bso', hidden_states, lilora_weight)
        return base + ALPHA * delta
    x = x + jnp.tanh(g_xattn[0]) * _L0_xattn_ref(ctx_1024, ctx_1024, _layernorm(x, axis=-1), L0_xattn_Wk_w, L0_xattn_Wk_b, L0_xattn_Wq_w, L0_xattn_Wq_b, L0_xattn_Wv_w, L0_xattn_Wv_b, L0_xattn_Wo_w, L0_xattn_Wo_b)
    x = x + jnp.tanh(g_ffn[0]) * _L0_ffn_ref(_layernorm(x, axis=-1), L0_ffn_w_gate, L0_ffn_w_up, L0_ffn_w_down)
    x = x + jnp.tanh(g_xattn[1]) * _L1_xattn_ref(_layernorm(x, axis=-1), ctx_1024, L1_xattn_Wq, L1_xattn_Wkv, L1_xattn_Wo)
    x = x + jnp.tanh(g_ffn[1]) * _L1_ffn_ref(_layernorm(x, axis=-1), L1_ffn_W, L1_ffn_b, L1_ffn_lora_down, L1_ffn_lora_up, L1_ffn_down_aux, L1_ffn_up_aux)
    return x

_drawn_inputs = setup_inputs


def setup_inputs(seed=0):
    import zlib

    import numpy as np

    out = dict(_drawn_inputs(seed))
    spreads = {'g_ffn': (-1.0, 0.6)}
    factors = {'L0_xattn_Wk_b': 8.0,
     'L0_xattn_Wq_b': 25.065,
     'L1_xattn_Wq': 59.649,
     'L1_xattn_Wkv': 51.91,
     'L1_xattn_Wo': 51.748,
     'L1_ffn_W': 64.0,
     'L1_ffn_b': 64.0,
     'L1_ffn_lora_down': 8.0,
     'L1_ffn_lora_up': 8.0,
     'L1_ffn_down_aux': 8.0,
     'L1_ffn_up_aux': 8.0}
    for name, (base, spread) in spreads.items():
        noise = np.random.default_rng([zlib.crc32(name.encode()), seed]).standard_normal(out[name].shape)
        drawn = base * np.exp(spread * noise) if base else spread * noise
        out[name] = jnp.asarray(drawn.astype(out[name].dtype))
    for name, factor in factors.items():
        out[name] = (out[name] * factor).astype(out[name].dtype)
    return out
```

```python
from contextlib import ExitStack

import numpy as np

import concourse.bass as bass
from concourse import mybir


B, S, SC, D = 64, 256, 120, 256
H, HD = 16, 16
HID = 768
P = 128
KC = D // P
NT = S // P
HC = HID // P
STAGES_BEHIND = 3
FRONT_X, FRONT_C = 1, 2
SCALE = float(np.float32(1.0 / 127.0))
EPS = 1e-5
SOFT = HD ** -0.5

F32 = mybir.dt.float32
F32R = mybir.dt.float32r
I32 = mybir.dt.int32
ALU = mybir.AluOpType
ACT = mybir.ActivationFunctionType
AX = mybir.AxisListType

SEG = {}
_at = 0
for _name, _cols in (("gate", KC * HID), ("up", KC * HID), ("down", HC * D),
                     ("q0", KC * D), ("q1", KC * D),
                     ("wo0", KC * D), ("wo1", KC * D), ("f1", KC * D)):
    SEG[_name] = _at
    _at += _cols
WCOLS = _at
CSEG = {"k0": 0, "v0": KC * D, "k1": 2 * KC * D, "v1": 2 * KC * D + KC * P}
CCOLS = 2 * KC * D + KC * P + KC * HD
ROUNDS = [("gate", KC * HID), ("up", KC * HID), ("down", HC * D), ("q0", 2 * KC * D), ("wo0", 2 * KC * D), ("f1", KC * D)]
STAGE = KC * HID
BIAS = {"q0": 0, "k0": D, "v0": 2 * D, "wo0": 3 * D, "f1": 4 * D}
NBIAS = 5 * D


def flamingo_kernel(nc, xp, cp, wc, wf, wi, brow, gates, cst, ldT, da, luT, uaT, out):
    iterations = out.shape[0]
    last_t = iterations
    ctx = ExitStack()
    with ctx:
        def sb(name, shape, dt=F32):
            return ctx.enter_context(nc.sbuf_tensor(name, shape, dt))

        def sem(name):
            return ctx.enter_context(nc.semaphore(name))

        w_hi = sb("w_hi", [P, WCOLS], F32R)
        w_lo = sb("w_lo", [P, WCOLS], F32R)
        ident = sb("ident", [P, P])
        masks = sb("masks", [P, 2])
        ones_pad = sb("ones_pad", [P, 64])
        neg_ident = sb("neg_ident", [P, P], F32R)
        neg_pick = sb("neg_pick", [P, 4 * P], F32R)
        w_ctx = sb("w_ctx", [P, CCOLS])
        ones_row = sb("ones_row", [1, P])
        bias_row = sb("bias_row", [1, 2 * D])
        ones2 = sb("ones2", [2, D], F32R)
        bias2 = sb("bias2", [2, NBIAS], F32R)
        minus_half = sb("minus_half", [P, NT])
        x_ln = sb("x_ln", [P, NT, D])
        x_res = sb("x_res", [P, NT, D])
        x1 = sb("x1", [P, NT, D])
        x2 = sb("x2", [P, NT, D])
        x3 = sb("x3", [P, NT, D])
        y_out = sb("y_out", [P, NT, D])
        xn = {s: sb(f"xn_{s}", [P, NT, D]) for s in "ABCD"}
        xt_hi = {s: sb(f"xt_hi_{s}", [P, KC, S], F32R) for s in "ABCD"}
        xt_lo = {s: sb(f"xt_lo_{s}", [P, KC, S], F32R) for s in "ABCD"}
        stats = {s: sb(f"stats_{s}", [P, NT, 6]) for s in "ABCD"}
        mv = {s: sb(f"mv_{s}", [P, NT, 2]) for s in "ABCD"}
        var_eps = {s: sb(f"var_eps_{s}", [P, NT]) for s in "ABCD"}
        ln_count = sb("ln_count", [P, 1])
        rstd = {s: sb(f"rstd_{s}", [P, NT]) for s in "ABCD"}
        ctx_f = {s: sb(f"ctx_f_{s}", [P, KC, P]) for s in "AC"}
        q0 = sb("q0", [P, KC, S])
        q1_hi = sb("q1_hi", [P, KC, S], F32R)
        q1_lo = sb("q1_lo", [P, KC, S], F32R)
        k0 = sb("k0", [P, KC, 2, P])
        k1_hi = sb("k1_hi", [P, 2, P], F32R)
        k1_lo = sb("k1_lo", [P, 2, P], F32R)
        v0_pad = sb("v0_pad", [P, H // 2, 64])
        v1_pad = sb("v1_pad", [P, 64])
        m0 = sb("m0", [P, 2, P], F32R)
        m1 = sb("m1", [P, 2, P])
        m1T = sb("m1T", [P, S], F32R)
        e0 = sb("e0", [P, NT, 4, 4, P])
        e1 = sb("e1", [P, KC, 4, 2, S])
        zt = sb("zt", [P, 8, P])
        z0 = sb("z0", [P, NT, P])
        rz0 = sb("rz0", [P, NT, P])
        rz1 = sb("rz1", [P, KC * S])
        y1f = sb("y1f", [P, KC * S])
        y_hi = {s: sb(f"y_hi_{s}", [P, KC, S], F32R) for s in "AC"}
        y_lo = {s: sb(f"y_lo_{s}", [P, KC, S], F32R) for s in "AC"}
        th = sb("th", [P, 2, S])
        act_g = sb("act_g", [P, 2, S])
        h_f = sb("h_f", [P, 2, S])
        h_hi = sb("h_hi", [P, HC, S], F32R)
        h_lo = sb("h_lo", [P, HC, S], F32R)
        e0_flat = e0[:, :, :, :, :].rearrange("p a b c d -> p (a b c d)")
        e1_flat = e1[:, :, :, :, :].rearrange("p a b c d -> p (a b c d)")
        stage = [e0_flat[:, 0:STAGE], e1_flat[:, 0:STAGE]]
        pick_f = e0_flat[:, STAGE:STAGE + 4 * P]
        b_f = e1_flat[0:1, STAGE:STAGE + NBIAS]
        small = STAGE + NBIAS
        da_s = e1_flat[0:100, small:small + D]
        uaT_s = e1_flat[0:50, small + D:small + 2 * D]
        t1_s = e1_flat[0:4, small + 2 * D:small + 3 * D]
        t2_s = e1_flat[0:50, small + 3 * D:small + 4 * D]
        ldT_s = e1_flat[0:100, small + 4 * D:small + 4 * D + 4]
        luT_s = e1_flat[0:4, small + 4 * D + 4:small + 4 * D + 54]
        b_hi = h_hi[0:1, :, :].rearrange("p a b -> p (a b)")[:, 0:NBIAS]
        b_lo = h_lo[0:1, :, :].rearrange("p a b -> p (a b)")[:, 0:NBIAS]
        tg = sb("tg", [P, 4])
        graw = sb("graw", [P, 4])

        scores = ctx.enter_context(nc.psum_tensor("scores", [P, 4, 512], F32))
        W = [ctx.enter_context(nc.psum_tensor(f"work{i}", [P, 512], F32)) for i in range(4)]

        names = []
        names += ["ld_cst", "ld_w0", "ld_w1", "w_scaled", "w_hi", "w_lo", "tg", "b_scaled", "b_split", "ld_bias2",
                  "li_t1", "li_t1s", "li_t2", "li_t2s", "li", "cst_r", "dequantised", "init_dve", "init_pool"]
        names += ["ld_ctx_C", "ld_ctx_A", "ld_x_ln", "ld_x_res", "st_out"]
        names += [f"{p}_{s}" for p in ("ln_mom", "ln_eps", "ln_rstd", "ln", "T_mm", "T_hi", "T_lo")
                  for s in "ABCD"]
        names += ["kv1_mm", "k1_hi", "v1_pad", "k1_lo", "k0_mm", "k0", "v0_mm", "v0_pad",
                  "q_mm_A", "q0", "q_mm_C", "q_hi_C", "q_lo_C"]
        names += ["M0_mm", "M1_mm", "M0_max", "M1_max", "mT_mm", "mT"]
        names += [f"T{c}_{p}" for c in (0, 1) for p in ("mm", "exp")]
        names += [f"A{c}_{p}" for c in (0, 1) for p in ("mm", "max", "sub", "exp", "z", "rz", "p")]
        names += ["z_part"]
        names += ["yA_mm", "yA_hi", "yA_lo", "woA_mm", "res_A"]
        names += ["yC_mm", "zC_mm", "rzC", "yC", "yC_hi", "yC_lo", "woC_mm", "res_C"]
        names += [f"G{m}_{p}" for m in range(HC) for p in ("mm", "tanh", "a", "h", "hi", "lo")]
        names += ["dn_mm", "res_B", "f1_mm", "res_D"]
        s = {n: sem(n) for n in names}
        unprimed = names[:names.index("ld_ctx_C")] + ["ld_ctx_C", "ld_ctx_A", "ld_x_ln", "ld_x_res", "z_part"]
        primed = [n for n in names if n not in unprimed and not n.startswith("ln_mom")]

        def w(which, name, off, n):
            a = SEG[name] + off
            return (w_hi if which == "hi" else w_lo)[:, a:a + n]

        block = ctx.enter_context(nc.Block())

        @block.sync
        def _(sp):
            sp.dma_start(ident[:, :], cst[:, 0:P]).then_inc(s["ld_cst"], 16)
            sp.dma_start(masks[:, :], cst[:, P:P + 2]).then_inc(s["ld_cst"], 16)
            sp.dma_start(pick_f[:, :], cst[:, P + 2:P + 2 + 4 * P]).then_inc(s["ld_cst"], 16)
            sp.dma_start(ones_pad[:, :], cst[:, P + 2 + 4 * P:P + 66 + 4 * P]).then_inc(s["ld_cst"], 16)
            sp.dma_start(w_ctx[:, :], wc).then_inc(s["ld_cst"], 16)
            sp.dma_start(bias_row[:, :], brow[:, BIAS["k0"]:BIAS["k0"] + 2 * D]).then_inc(s["ld_cst"], 16)
            sp.dma_start(graw[:, :], gates).then_inc(s["ld_cst"], 16)
            sp.dma_start(b_f[:, :], brow).then_inc(s["ld_cst"], 16)
            sp.dma_start(ldT_s[:, :], ldT).then_inc(s["ld_cst"], 16)
            sp.dma_start(da_s[:, :], da).then_inc(s["ld_cst"], 16)
            sp.dma_start(luT_s[:, :], luT).then_inc(s["ld_cst"], 16)
            sp.dma_start(uaT_s[:, :], uaT).then_inc(s["ld_cst"], 16)
            for r, (name, n) in enumerate(ROUNDS):
                if r >= 2:
                    sp.wait_ge(s["w_lo"], r - 1)
                src = wi[:, SEG[name]:SEG[name] + n] if r < 3 else wf[:, SEG[name] - SEG["q0"]:SEG[name] - SEG["q0"] + n]
                dst = stage[r % 2][:, 0:n]
                sp.dma_start(dst.bitcast(I32) if r < 3 else dst, src).then_inc(s[f"ld_w{r % 2}"], 16)
            sp.wait_ge(s["b_split"], 2)
            sp.dma_start(bias2[0:1, :].bitcast(F32), b_hi.bitcast(F32)).then_inc(s["ld_bias2"], 16)
            sp.dma_start(bias2[1:2, :].bitcast(F32), b_lo.bitcast(F32)).then_inc(s["ld_bias2"], 16)
            for n in primed:
                sp.sem_inc(s[n], 16 if n == "st_out" else 1)
            sp.wait_ge(s["init_dve"], 1)
            with nc.sync.Fori(2, last_t + 2) as t:
                sp.wait_ge(s["kv1_mm"], t - 1)
                sp.dma_start(ctx_f["C"][:, :, :], cp[t - 2, :, :, :]).then_inc(s["ld_ctx_C"], 16)
                sp.wait_ge(s["v0_mm"], t - 1)
                sp.dma_start(ctx_f["A"][:, :, :], cp[t, :, :, :]).then_inc(s["ld_ctx_A"], 16)
                sp.wait_ge(s["ln_A"], t - 1)
                sp.dma_start(x_ln[:, :, :], xp[t - 1, :, :].rearrange("(i p) d -> p i d", p=P)).then_inc(s["ld_x_ln"], 16)
                sp.wait_ge(s["res_A"], t - 1)
                sp.dma_start(x_res[:, :, :], xp[t - 2, :, :].rearrange("(i p) d -> p i d", p=P)).then_inc(s["ld_x_res"], 16)
                sp.wait_ge(s["res_D"], t)
                sp.dma_start(out[t - 2, :, :].rearrange("(i p) d -> p i d", p=P), y_out[:, :, :]).then_inc(s["st_out"], 16)
            sp.wait_ge(s["st_out"], 16 * (last_t + 1))

        @block.gpsimd
        def _(pool):
            pool.memset(minus_half[:, :], -0.5).then_inc(s["init_pool"], 1)
            pool.memset(v0_pad[:, :, :], 0.0).then_inc(s["init_pool"], 1)
            pool.memset(v1_pad[:, :], 0.0).then_inc(s["init_pool"], 1)
            pool.memset(ones2[:, :].bitcast(F32), 1.0).then_inc(s["init_pool"], 1)
            pool.memset(ones_row[:, :], 1.0).then_inc(s["init_pool"], 1)
            pool.wait_ge(s["init_pool"], 5)

            def root(st, t):
                pool.wait_ge(s[f"ln_eps_{st}"], t)
                pool.wait_ge(s[f"ln_{st}"], t - 1)
                pool.tensor_tensor(rstd[st][:, :], var_eps[st][:, :], minus_half[:, :], ALU.pow)\
                    .then_inc(s[f"ln_rstd_{st}"], 1)

            def hidden_lo(m, t):
                pool.wait_ge(s[f"G{m}_hi"], t)
                pool.tensor_tensor(h_lo[:, m, :], h_f[:, m % 2, :], h_hi[:, m, :].bitcast(F32), ALU.subtract)\
                    .then_inc(s[f"G{m}_lo"], 1)

            def sum_heads(c, t):
                e = e0[0:SC, c, :, :, :].rearrange("p a b n -> p (a b) n")
                pool.wait_ge(s[f"A{c}_exp"], t)
                if c == 1:
                    pool.wait_ge(s["A0_z"], t)
                else:
                    pool.wait_ge(s["A1_z"], t - 1)
                pool.tensor_tensor(zt[0:SC, :, :], e[:, 0:8, :], e[:, 8:16, :], ALU.add).then_inc(s["z_part"], 1)
                pool.wait_ge(s["z_part"], 6 * (t - 2) + 3 * c + 1)
                pool.tensor_tensor(zt[0:SC, 0:4, :], zt[0:SC, 0:4, :], zt[0:SC, 4:8, :], ALU.add)\
                    .then_inc(s["z_part"], 1)
                pool.wait_ge(s["z_part"], 6 * (t - 2) + 3 * c + 2)
                pool.tensor_tensor(zt[0:SC, 0:2, :], zt[0:SC, 0:2, :], zt[0:SC, 2:4, :], ALU.add)\
                    .then_inc(s["z_part"], 1)
                pool.wait_ge(s["z_part"], 6 * (t - 2) + 3 * c + 3)
                pool.tensor_tensor(z0[0:SC, c, :], zt[0:SC, 0, :], zt[0:SC, 1, :], ALU.add).then_inc(s[f"A{c}_z"], 1)

            with nc.gpsimd.Fori(2, last_t + 2) as t:
                root("A", t)
                root("B", t)
                for m in range(4):
                    hidden_lo(m, t)
                pool.wait_ge(s["yC_hi"], t)
                pool.tensor_tensor(y_lo["C"][:, :, :], y1f[:, :].rearrange("p (k n) -> p k n", k=KC),
                                   y_hi["C"][:, :, :].bitcast(F32), ALU.subtract).then_inc(s["yC_lo"], 1)
                sum_heads(0, t)
                hidden_lo(4, t)
                root("D", t)
                hidden_lo(5, t)
                sum_heads(1, t)
                root("C", t)

        @block.scalar
        def _(act):
            act.wait_ge(s["ld_cst"], 16 * 12)
            act.activation(tg[:, :], graw[:, :], ACT.Tanh).then_inc(s["tg"], 1)
            act.activation(neg_ident[:, :], ident[:, :], ACT.Copy, scale=-1.0).then_inc(s["cst_r"], 1)
            act.activation(neg_pick[:, :], pick_f[:, :], ACT.Copy).then_inc(s["cst_r"], 1)
            act.wait_ge(s["b_scaled"], 2)
            act.activation(b_hi[:, :], b_f[:, :], ACT.Copy).then_inc(s["b_split"], 1)
            for r, (name, n) in enumerate(ROUNDS):
                act.wait_ge(s["w_scaled"], r + 1)
                act.activation(w_hi[:, SEG[name]:SEG[name] + n], stage[r % 2][:, 0:n], ACT.Copy).then_inc(s["w_hi"], 1)
            act.wait_ge(s["init_pool"], 5)
            act.wait_ge(s["init_dve"], 1)

            def split_hi(out, src, name):
                return act.activation(out, src, ACT.Copy).then_inc(s[name], 1)

            def transposed_hi(st, bank, readers, t):
                act.wait_ge(s[f"T_mm_{st}"], t)
                act.wait_ge(s[readers], t - 1)
                split_hi(xt_hi[st][:, :, :], W[bank][:, :].rearrange("p (k n) -> p k n", k=KC), f"T_hi_{st}")

            def tanh(m, bank, t):
                act.wait_ge(s[f"G{m}_mm"], t)
                if m >= 2:
                    act.wait_ge(s[f"G{m - 2}_a"], t)
                else:
                    act.wait_ge(s[f"G{m + 4}_a"], t - 1)
                act.activation(th[:, m % 2, :], W[bank][:, 0:S], ACT.Tanh, scale=0.5).then_inc(s[f"G{m}_tanh"], 1)

            def hidden_hi(m, t):
                act.wait_ge(s[f"G{m}_h"], t)
                act.wait_ge(s["dn_mm"], t - 1)
                split_hi(h_hi[:, m, :], h_f[:, m % 2, :], f"G{m}_hi")

            def exps(e, c, name, readers, t):
                for half in range(2):
                    last = act.activation(e[0:SC, c, 2 * half:2 * half + 2, :, :].rearrange("p a b n -> p (a b n)"),
                                   scores[0:SC, 2 * half:2 * half + 2, :].rearrange("p a n -> p (a n)"),
                                   ACT.Exp, scale=SOFT)
                last.then_inc(s[f"{name}_exp"], 1)

            with nc.scalar.Fori(2, last_t + 2) as t:
                act.wait_ge(s["kv1_mm"], t)
                act.wait_ge(s["T1_mm"], t - 1)
                act.activation(k1_hi[:, 0, :], W[0][:, 0:P], ACT.Copy, scale=masks[:, 0:1])
                act.activation(k1_hi[:, 1, :], W[0][:, 0:P], ACT.Copy, scale=masks[:, 1:2]).then_inc(s["k1_hi"], 1)
                act.wait_ge(s["zC_mm"], t - 1)
                act.activation(v1_pad[0:SC, 0:HD], W[0][0:SC, P:P + HD], ACT.Copy)
                act.activation(v1_pad[0:SC, 48:48 + HD], W[0][0:SC, P:P + HD], ACT.Copy).then_inc(s["v1_pad"], 1)
                act.wait_ge(s["k0_mm"], t)
                act.wait_ge(s["A1_mm"], t - 1)
                for par in range(2):
                    last = act.activation(k0[:, :, par, :], W[1][:, 0:KC * P].rearrange("p (k n) -> p k n", k=KC),
                                          ACT.Copy, scale=masks[:, par:par + 1])
                last.then_inc(s["k0"], 1)
                transposed_hi("A", 2, "q_mm_A", t)
                transposed_hi("D", 0, "f1_mm", t)
                act.wait_ge(s["q_mm_A"], t)
                act.wait_ge(s["A1_mm"], t - 1)
                split_hi(q0[:, :, :], W[1][:, :].rearrange("p (k n) -> p k n", k=KC), "q0")
                transposed_hi("C", 3, "q_mm_C", t)
                act.wait_ge(s["q_mm_C"], t)
                act.wait_ge(s["T1_mm"], t - 1)
                split_hi(q1_hi[:, :, :], W[0][:, :].rearrange("p (k n) -> p k n", k=KC), "q_hi_C")
                act.wait_ge(s["yA_mm"], t)
                act.wait_ge(s["woA_mm"], t - 1)
                split_hi(y_hi["A"][:, :, :], W[1][:, :].rearrange("p (k n) -> p k n", k=KC), "yA_hi")
                act.wait_ge(s["v0_mm"], t)
                v_src = W[2][0:SC, 0:D].rearrange("p (g r j) -> p g r j", r=2, j=HD)
                act.activation(v0_pad[0:SC, :, 0:HD], v_src[:, :, 0, :], ACT.Copy)
                act.activation(v0_pad[0:SC, :, 48:48 + HD], v_src[:, :, 1, :], ACT.Copy).then_inc(s["v0_pad"], 1)
                transposed_hi("B", 0, "G5_mm", t)
                act.wait_ge(s["mT_mm"], t)
                act.wait_ge(s["T1_mm"], t - 1)
                act.activation(m1T[:, :], W[1][:, 0:S], ACT.Copy).then_inc(s["mT"], 1)
                tanh(0, 2, t)
                tanh(1, 3, t)
                hidden_hi(0, t)
                act.wait_ge(s["T0_mm"], t)
                act.wait_ge(s["zC_mm"], t - 1)
                exps(e1, 0, "T0", None, t)
                tanh(2, 0, t)
                hidden_hi(1, t)
                act.wait_ge(s["T1_mm"], t)
                exps(e1, 1, "T1", None, t)
                tanh(3, 1, t)
                hidden_hi(2, t)
                hidden_hi(3, t)
                act.wait_ge(s["A0_sub"], t)
                exps(e0, 0, "A0", None, t)
                tanh(4, 0, t)
                act.wait_ge(s["yC"], t)
                act.wait_ge(s["woC_mm"], t - 1)
                split_hi(y_hi["C"][:, :, :], y1f[:, :].rearrange("p (k n) -> p k n", k=KC), "yC_hi")
                hidden_hi(4, t)
                tanh(5, 2, t)
                act.wait_ge(s["A1_sub"], t)
                exps(e0, 1, "A1", None, t)
                hidden_hi(5, t)

        @block.vector
        def _(dve):
            dve.wait_ge(s["tg"], 1)
            dve.tensor_scalar(b_f[:, BIAS["wo0"]:BIAS["wo0"] + D], b_f[:, BIAS["wo0"]:BIAS["wo0"] + D],
                              tg[0:1, 0:1], None, ALU.mult).then_inc(s["b_scaled"], 1)
            dve.tensor_scalar(b_f[:, BIAS["f1"]:BIAS["f1"] + D], b_f[:, BIAS["f1"]:BIAS["f1"] + D],
                              tg[0:1, 3:4], None, ALU.mult).then_inc(s["b_scaled"], 1)
            dve.wait_ge(s["b_split"], 1)
            dve.tensor_tensor(b_lo[:, :], b_f[:, :], b_hi[:, :].bitcast(F32), ALU.subtract).then_inc(s["b_split"], 1)
            for r, (name, n) in enumerate(ROUNDS):
                st = stage[r % 2][:, 0:n]
                dve.wait_ge(s[f"ld_w{r % 2}"], 16 * (r // 2 + 1))
                if name in ("gate", "up"):
                    dve.tensor_scalar(st, st.bitcast(I32), SCALE, None, ALU.mult).then_inc(s["w_scaled"], 1)
                elif name == "down":
                    dve.tensor_scalar(st, st.bitcast(I32), SCALE, None, ALU.mult).then_inc(s["dequantised"], 1)
                    dve.wait_ge(s["dequantised"], 1)
                    dve.tensor_scalar(st, st, tg[:, 2:3], 0.5, ALU.mult, ALU.mult).then_inc(s["w_scaled"], 1)
                elif name == "wo0":
                    dve.tensor_scalar(st[:, 0:KC * D], st[:, 0:KC * D], tg[:, 0:1], None, ALU.mult)
                    dve.tensor_scalar(st[:, KC * D:], st[:, KC * D:], tg[:, 1:2], None, ALU.mult)\
                        .then_inc(s["w_scaled"], 1)
                elif name == "f1":
                    dve.wait_ge(s["li_t1"], 1)
                    dve.tensor_copy(t1_s[:, :], W[0][0:4, 0:D]).then_inc(s["li_t1s"], 1)
                    dve.wait_ge(s["li_t2"], 1)
                    dve.tensor_copy(t2_s[:, :], W[1][0:50, 0:D]).then_inc(s["li_t2s"], 1)
                    dve.wait_ge(s["li"], 1)
                    dve.tensor_tensor(st, W[2][:, :], st, ALU.add).then_inc(s["li_t2s"], 1)
                    dve.wait_ge(s["li_t2s"], 2)
                    dve.tensor_scalar(st, st, tg[:, 3:4], None, ALU.mult).then_inc(s["w_scaled"], 1)
                else:
                    dve.engine_nop().then_inc(s["w_scaled"], 1)
                dve.wait_ge(s["w_hi"], r + 1)
                dve.tensor_tensor(w_lo[:, SEG[name]:SEG[name] + n], st, w_hi[:, SEG[name]:SEG[name] + n].bitcast(F32),
                                  ALU.subtract).then_inc(s["w_lo"], 1)
            dve.wait_ge(s["w_lo"], len(ROUNDS))
            for tile in (x1, x2, x3, xn["B"], xn["C"], xn["D"], m1[:, :, :]):
                dve.memset(tile[:, :, :], 0.0)
            dve.memset(e0[:, :, :, :, :], 0.0).then_inc(s["init_dve"], 1)

            def ln_stats(st, x, t):
                for i in range(NT):
                    last = dve.bn_stats(stats[st][:, i, :], x[:, i, :])
                last.then_inc(s[f"ln_mom_{st}"], 1)
                dve.wait_ge(s[f"ln_mom_{st}"], 2 * t - 3)
                dve.tensor_copy(ln_count[:, :], stats[st][:, 0, 0:1])
                for i in range(NT):
                    last = dve.bn_aggr(mv[st][:, i, :], stats[st][:, i, :])
                last.then_inc(s[f"ln_mom_{st}"], 1)
                dve.wait_ge(s[f"ln_mom_{st}"], 2 * t - 2)
                dve.tensor_scalar(var_eps[st][:, :], mv[st][:, :, 1], EPS, None, ALU.add).then_inc(s[f"ln_eps_{st}"], 1)

            def ln_apply(st, x, t):
                dve.wait_ge(s[f"ln_rstd_{st}"], t)
                for i in range(NT):
                    last = dve.tensor_scalar(xn[st][:, i, :], x[:, i, :], mv[st][:, i, 0:1], rstd[st][:, i:i + 1],
                                             ALU.subtract, ALU.mult)
                last.then_inc(s[f"ln_{st}"], 1)

            def low(out, src, hi, name):
                return dve.tensor_tensor(out, src, hi.bitcast(F32), ALU.subtract).then_inc(s[name], 1)

            def transposed_lo(st, bank, t):
                dve.wait_ge(s[f"T_hi_{st}"], t)
                low(xt_lo[st][:, :, :], W[bank][:, :].rearrange("p (k n) -> p k n", k=KC), xt_hi[st][:, :, :],
                    f"T_lo_{st}")

            def gated(m, bank, t):
                dve.wait_ge(s[f"G{m}_tanh"], t)
                dve.scalar_tensor_tensor(act_g[:, m % 2, :], th[:, m % 2, :], 1.0, W[bank][:, 0:S],
                                         ALU.add, ALU.mult).then_inc(s[f"G{m}_a"], 1)
                dve.wait_ge(s[f"G{m}_a"], t)
                if m >= 2:
                    dve.wait_ge(s[f"G{m - 2}_lo"], t)
                else:
                    dve.wait_ge(s[f"G{m + 4}_lo"], t - 1)
                dve.tensor_tensor(h_f[:, m % 2, :], W[bank][:, S:2 * S], act_g[:, m % 2, :], ALU.mult)\
                    .then_inc(s[f"G{m}_h"], 1)

            def head_max(c, t):
                dve.wait_ge(s[f"A{c}_mm"], t)
                dve.tensor_reduce(m0[0:SC, c, :], scores[0:SC, :, :].rearrange("p r (h n) -> p n (r h)", n=P),
                                  AX.X, ALU.max).then_inc(s[f"A{c}_max"], 1)

            def key_max(c, t):
                dve.wait_ge(s[f"M{c}_mm"], t)
                dve.wait_ge(s["mT_mm"], t - 1)
                dve.tensor_reduce(m1[:, c, :].rearrange("p (r j) -> p r j", r=4)[:, :, 0:4],
                                  scores[:, :, :].rearrange("p r (h n) -> p r h n", n=P)[:, :, :, 0:SC],
                                  AX.X, ALU.max).then_inc(s[f"M{c}_max"], 1)

            def normalise(c, t):
                dve.wait_ge(s[f"A{c}_z"], t)
                dve.reciprocal(rz0[0:SC, c, :], z0[0:SC, c, :]).then_inc(s[f"A{c}_rz"], 1)
                dve.wait_ge(s[f"A{c}_rz"], t)
                e = e0[0:SC, c, :, :, :].rearrange("p a b n -> p (a b) n")
                dve.tensor_tensor(e, e, rz0[0:SC, c:c + 1, :].to_broadcast([SC, H, P]), ALU.mult)\
                    .then_inc(s[f"A{c}_p"], 1)

            def residual(out, x, bank, mm, name, t):
                dve.wait_ge(s[mm], t)
                dve.tensor_tensor(out[:, :, :], W[bank][:, :].rearrange("p (i d) -> p i d", i=NT), x[:, :, :], ALU.add)\
                    .then_inc(s[name], 1)
                dve.wait_ge(s[name], t)

            with nc.vector.Fori(2, last_t + 2) as t:
                dve.wait_ge(s["ld_x_ln"], 16 * (t - 1))
                ln_stats("A", x_ln, t)
                dve.wait_ge(s["k1_hi"], t)
                dve.wait_ge(s["v1_pad"], t)
                for par in range(2):
                    last = dve.scalar_tensor_tensor(k1_lo[:, par, :], W[0][:, 0:P], masks[:, par:par + 1],
                                                    k1_hi[:, par, :].bitcast(F32), ALU.mult, ALU.subtract)
                last.then_inc(s["k1_lo"], 1)
                ln_apply("A", x_ln, t)
                transposed_lo("A", 2, t)
                transposed_lo("D", 0, t)
                dve.wait_ge(s["st_out"], 16 * (t - 1))
                residual(y_out, x3, 2, "f1_mm", "res_D", t)
                transposed_lo("C", 3, t)
                dve.wait_ge(s["q_hi_C"], t)
                low(q1_lo[:, :, :], W[0][:, :].rearrange("p (k n) -> p k n", k=KC), q1_hi[:, :, :], "q_lo_C")
                dve.wait_ge(s["yA_hi"], t)
                low(y_lo["A"][:, :, :], W[1][:, :].rearrange("p (k n) -> p k n", k=KC), y_hi["A"][:, :, :], "yA_lo")
                key_max(0, t)
                dve.wait_ge(s["ld_x_res"], 16 * (t - 1))
                residual(x1, x_res, 3, "woA_mm", "res_A", t)
                ln_stats("B", x1, t)
                key_max(1, t)
                ln_apply("B", x1, t)
                transposed_lo("B", 0, t)
                gated(0, 2, t)
                gated(1, 3, t)
                gated(2, 0, t)
                gated(3, 1, t)
                head_max(0, t)
                dve.wait_ge(s["zC_mm"], t)
                dve.reciprocal(rz1[:, :], W[3][:, :]).then_inc(s["rzC"], 1)
                dve.wait_ge(s["rzC"], t)
                dve.wait_ge(s["yC_mm"], t)
                dve.tensor_tensor(y1f[:, :], W[2][:, :], rz1[:, :], ALU.mult).then_inc(s["yC"], 1)
                gated(4, 0, t)
                residual(x3, x2, 1, "woC_mm", "res_C", t)
                ln_stats("D", x3, t)
                normalise(0, t)
                ln_apply("D", x3, t)
                head_max(1, t)
                gated(5, 2, t)
                residual(x2, x1, 3, "dn_mm", "res_B", t)
                ln_stats("C", x2, t)
                normalise(1, t)
                ln_apply("C", x2, t)

        @block.tensor
        def _(pe):
            pe.wait_ge(s["ld_cst"], 16 * 12)
            pe.matmul(W[0][0:4, 0:D], ldT_s[:, :], da_s[:, :], start=True, stop=True).then_inc(s["li_t1"], 1)
            pe.wait_ge(s["li_t1s"], 1)
            pe.matmul(W[1][0:50, 0:D], luT_s[:, :], t1_s[:, :], start=True, stop=True).then_inc(s["li_t2"], 1)
            pe.wait_ge(s["li_t2s"], 1)
            for kc in range(KC):
                last = pe.matmul(W[2][:, kc * D:(kc + 1) * D], t2_s[:, kc * P:(kc + 1) * P], uaT_s[:, :],
                                 start=True, stop=True)
            last.then_inc(s["li"], 1)
            pe.wait_ge(s["w_lo"], len(ROUNDS))
            pe.wait_ge(s["ld_bias2"], 32)
            pe.wait_ge(s["cst_r"], 2)
            pe.wait_ge(s["init_pool"], 5)
            pe.wait_ge(s["init_dve"], 1)

            def product(out, terms, bias=None):
                first = True
                for n, ((a_hi, a_lo), (b_hi_, b_lo_)) in enumerate(terms):
                    end = n == len(terms) - 1 and bias is None
                    pe.matmul(out, a_hi, b_hi_, start=first, stop=False)
                    pe.matmul(out, a_hi, b_lo_, start=False, stop=False)
                    last = pe.matmul(out, a_lo, b_hi_, start=False, stop=end)
                    first = False
                if bias is not None:
                    last = pe.matmul(out, bias[0], bias[1], start=False, stop=True)
                return last

            def pair(hi, lo, *index):
                return hi[index], lo[index]

            def wpair(name, off, n):
                return w("hi", name, off, n), w("lo", name, off, n)

            def wc_of(name, off, n):
                return w_ctx[:, CSEG[name] + off:CSEG[name] + off + n]

            def transposes(st, bank):
                for i in range(NT):
                    for kc in range(KC):
                        last = pe.transpose(W[bank][:, kc * S + i * P:kc * S + (i + 1) * P],
                                            xn[st][:, i, kc * P:(kc + 1) * P], ident[:, :])
                return last.then_inc(s[f"T_mm_{st}"], 1)

            def queries(st, bank, name, bias):
                for oc in range(KC):
                    last = product(W[bank][:, oc * S:(oc + 1) * S],
                                   [(wpair(name, kc * D + oc * P, P), (xt_hi[st][:, kc, :], xt_lo[st][:, kc, :]))
                                    for kc in range(KC)],
                                   (bias2[:, BIAS[name] + oc * P:BIAS[name] + (oc + 1) * P], ones2[:, 0:S])
                                   if bias else None)
                return last.then_inc(s[f"q_mm_{st}"], 1)

            def rows_out(bank, a_hi, a_lo, name, chunks, bias=False):
                for i in range(NT):
                    last = product(W[bank][:, i * D:(i + 1) * D],
                                   [((a_hi[:, kc, i * P:(i + 1) * P], a_lo[:, kc, i * P:(i + 1) * P]),
                                     wpair(name, kc * D, D)) for kc in range(chunks)],
                                   (ones2[:, 0:P], bias2[:, BIAS[name]:BIAS[name] + D]) if bias else None)
                return last

            def gate_up(m, bank, t):
                for half, name in ((0, "gate"), (1, "up")):
                    last = product(W[bank][:, half * S:(half + 1) * S],
                                   [(wpair(name, kc * HID + m * P, P), (xt_hi["B"][:, kc, :], xt_lo["B"][:, kc, :]))
                                    for kc in range(KC)])
                last.then_inc(s[f"G{m}_mm"], 1)

            def key_scores(c):
                for r in range(4):
                    for cc in range(KC):
                        last = pe.matmul(scores[:, r, cc * 2 * P:(cc + 1) * 2 * P],
                                         q1_hi[32 * r:32 * r + 32, cc, c * P:(c + 1) * P],
                                         k1_hi[32 * r:32 * r + 32, :, :].rearrange("p a n -> p (a n)"),
                                         start=True, stop=True)
                last.then_inc(s[f"M{c}_mm"], 1)

            def scores0(c):
                for r in range(4):
                    for cc in range(KC):
                        for par in range(2):
                            j = 2 * cc + par
                            last = pe.matmul(scores[:, r, j * P:(j + 1) * P], k0[32 * r:32 * r + 32, cc, par, :],
                                             q0[32 * r:32 * r + 32, cc, c * P:(c + 1) * P],
                                             start=j == 0, stop=False, skip_group_check=True)
                last.then_inc(s[f"A{c}_mm"], 1)

            def scores1(cc):
                for r in range(4):
                    rows = slice(32 * r, 32 * r + 32)
                    for par in range(2):
                        j = 2 * cc + par
                        o = scores[:, r, par * S:(par + 1) * S]
                        pe.matmul(o, k1_hi[rows, par, :], q1_hi[rows, cc, :], start=True, stop=False)
                        pe.matmul(o, k1_hi[rows, par, :], q1_lo[rows, cc, :], start=False, stop=False)
                        pe.matmul(o, k1_lo[rows, par, :], q1_hi[rows, cc, :], start=False, stop=False)
                        last = pe.matmul(o, neg_pick[rows, j * P:(j + 1) * P], m1T[rows, :], start=False, stop=True)
                last.then_inc(s[f"T{cc}_mm"], 1)

            def subtract_max(c, t):
                pe.wait_ge(s[f"A{c}_max"], t)
                for r in range(4):
                    last = pe.matmul(scores[:, r, :].rearrange("p (h n) -> p h n", n=P), neg_ident[0:SC, :],
                                     m0[0:SC, c:c + 1, :].to_broadcast([SC, 4, P]), start=False, stop=True,
                                     skip_group_check=True)
                last.then_inc(s[f"A{c}_sub"], 1)

            def per_head(bank, v_of, cc, e_of, query, n):
                for par in range(2):
                    for r in range(4):
                        last = pe.matmul(W[bank][32 * r:32 * r + 32, cc * S + query:cc * S + query + n],
                                         v_of(4 * cc + r, par), e_of(r, par), start=par == 0, stop=par == 1)
                return last

            with nc.tensor.Fori(2, last_t + 2) as t:
                pe.wait_ge(s["ld_ctx_C"], 16 * (t - 1))
                pe.wait_ge(s["G4_h"], t - 1)
                for kc in range(KC):
                    pe.matmul(W[0][:, 0:P], wc_of("k1", kc * P, P), ctx_f["C"][:, kc, :],
                              start=kc == 0, stop=kc == KC - 1)
                for kc in range(KC):
                    last = pe.matmul(W[0][:, P:P + HD], ctx_f["C"][:, kc, :], wc_of("v1", kc * HD, HD),
                                     start=kc == 0, stop=kc == KC - 1)
                last.then_inc(s["kv1_mm"], 1)
                pe.wait_ge(s["ld_ctx_A"], 16 * (t - 1))
                pe.wait_ge(s["res_C"], t - 1)
                for oc in range(KC):
                    for kc in range(KC):
                        pe.matmul(W[1][:, oc * P:(oc + 1) * P], wc_of("k0", kc * D + oc * P, P), ctx_f["A"][:, kc, :],
                                  start=kc == 0, stop=False)
                    last = pe.matmul(W[1][:, oc * P:(oc + 1) * P], bias_row[:, oc * P:(oc + 1) * P], ones_row[:, :],
                                     start=False, stop=True)
                last.then_inc(s["k0_mm"], 1)
                pe.wait_ge(s["ln_A"], t)
                pe.wait_ge(s["G5_h"], t - 1)
                transposes("A", 2)
                pe.wait_ge(s["k1_lo"], t)
                pe.wait_ge(s["v1_pad"], t)
                pe.wait_ge(s["ln_D"], t - 1)
                transposes("D", 0)
                pe.wait_ge(s["T_lo_A"], t)
                pe.wait_ge(s["k0"], t)
                queries("A", 1, "q0", True)
                pe.wait_ge(s["T_lo_D"], t)
                rows_out(2, xt_hi["D"], xt_lo["D"], "f1", KC, True).then_inc(s["f1_mm"], 1)
                pe.wait_ge(s["ln_C"], t - 1)
                pe.wait_ge(s["res_B"], t - 1)
                transposes("C", 3)
                pe.wait_ge(s["T_lo_C"], t)
                queries("C", 0, "q1", False)
                pe.wait_ge(s["A1_p"], t - 1)
                pe.wait_ge(s["v0_pad"], t - 1)
                pe.wait_ge(s["q0"], t)
                for c in range(NT):
                    for cc in range(KC):
                        last = per_head(1, lambda g, par: v0_pad[0:SC, g, 32 * par:32 * par + 32], cc,
                                        lambda r, par: e0[0:SC, c, r, 2 * cc + par, :], c * P, P)
                last.then_inc(s["yA_mm"], 1)
                pe.wait_ge(s["q_hi_C"], t)
                pe.wait_ge(s["k1_hi"], t)
                pe.wait_ge(s["A1_exp"], t - 1)
                key_scores(0)
                pe.wait_ge(s["res_D"], t)
                for kc in range(KC):
                    pe.matmul(W[2][:, 0:D], ctx_f["A"][:, kc, :], wc_of("v0", kc * D, D), start=kc == 0, stop=False)
                pe.matmul(W[2][:, 0:D], ones_row[:, :], bias_row[:, D:2 * D], start=False, stop=True)\
                    .then_inc(s["v0_mm"], 1)
                pe.wait_ge(s["yA_lo"], t)
                rows_out(3, y_hi["A"], y_lo["A"], "wo0", KC, True).then_inc(s["woA_mm"], 1)
                pe.wait_ge(s["M0_max"], t)
                key_scores(1)
                pe.wait_ge(s["ln_B"], t)
                transposes("B", 0)
                pe.wait_ge(s["M1_max"], t)
                for c in range(NT):
                    last = pe.transpose(W[1][:, c * P:(c + 1) * P], m1[:, c, :], ident[:, :])
                last.then_inc(s["mT_mm"], 1)
                pe.wait_ge(s["T_lo_B"], t)
                pe.wait_ge(s["v0_pad"], t)
                gate_up(0, 2, t)
                gate_up(1, 3, t)
                pe.wait_ge(s["mT"], t)
                pe.wait_ge(s["k1_lo"], t)
                pe.wait_ge(s["q_lo_C"], t)
                scores1(0)
                gate_up(2, 0, t)
                pe.wait_ge(s["T0_exp"], t)
                scores1(1)
                gate_up(3, 1, t)
                pe.wait_ge(s["T1_exp"], t)
                scores0(0)
                pe.wait_ge(s["G0_h"], t)
                for cc in range(KC):
                    last = per_head(2, lambda g, par: v1_pad[0:SC, 32 * par:32 * par + 32], cc,
                                    lambda r, par: e1[0:SC, cc, r, par, :], 0, S)
                last.then_inc(s["yC_mm"], 1)
                pe.wait_ge(s["G1_h"], t)
                for cc in range(KC):
                    last = per_head(3, lambda g, par: ones_pad[0:SC, 32 * par:32 * par + 32], cc,
                                    lambda r, par: e1[0:SC, cc, r, par, :], 0, S)
                last.then_inc(s["zC_mm"], 1)
                subtract_max(0, t)
                pe.wait_ge(s["G2_h"], t)
                gate_up(4, 0, t)
                pe.wait_ge(s["yC_lo"], t)
                pe.wait_ge(s["G3_h"], t)
                rows_out(1, y_hi["C"], y_lo["C"], "wo1", KC).then_inc(s["woC_mm"], 1)
                pe.wait_ge(s["A0_exp"], t)
                scores0(1)
                gate_up(5, 2, t)
                subtract_max(1, t)
                for m in range(HC):
                    pe.wait_ge(s[f"G{m}_lo"], t)
                rows_out(3, h_hi, h_lo, "down", HC).then_inc(s["dn_mm"], 1)


def kernel(**inputs):
    import concourse.bacc as bacc
    from concourse.bass_utils import run_bass_kernel_spmd

    a = {k: np.asarray(v) for k, v in inputs.items()}
    x, c = a["x"], a["ctx_1024"]
    batches = x.shape[0]
    T = batches + STAGES_BEHIND
    f = x.dtype

    def chunks(m):
        return m.reshape(-1, P, m.shape[1]).transpose(1, 0, 2).reshape(P, -1)

    perm = np.arange(D).reshape(HD, H).T.reshape(-1)
    xp = np.concatenate([np.zeros((FRONT_X, S, D), f), x, np.zeros((T - batches, S, D), f)])
    ct = c.transpose(0, 2, 1).reshape(batches, KC, P, SC).transpose(0, 2, 1, 3)
    cpad = np.zeros((FRONT_C + T, P, KC, P), f)
    cpad[FRONT_C:FRONT_C + batches, :, :, :SC] = ct
    wc = np.concatenate([
        chunks(a["L0_xattn_Wk_w"].T[:, perm]), chunks(a["L0_xattn_Wv_w"].T[:, perm]),
        chunks(np.tile(a["L1_xattn_Wkv"][:, :HD], (1, P // HD))), chunks(a["L1_xattn_Wkv"][:, HD:])], axis=1)
    wf = np.concatenate([
        chunks(a["L0_xattn_Wq_w"].T[:, perm]), chunks(a["L1_xattn_Wq"]),
        chunks(a["L0_xattn_Wo_w"].T[perm]), chunks(a["L1_xattn_Wo"]), chunks(a["L1_ffn_W"].T)], axis=1)
    wi = np.concatenate([chunks(a["L0_ffn_w_gate"].T), chunks(a["L0_ffn_w_up"].T), chunks(a["L0_ffn_w_down"].T)], axis=1)
    brow = np.concatenate([a["L0_xattn_Wq_b"][perm], a["L0_xattn_Wk_b"][perm], a["L0_xattn_Wv_b"][perm],
                           a["L0_xattn_Wo_b"], a["L1_ffn_b"]])[None]
    gates = np.tile(np.concatenate([a["g_xattn"], a["g_ffn"]])[None], (P, 1))
    parity = (np.arange(P) // HD) % 2
    pick = np.zeros((P, 4, P), f)
    for r in range(4):
        for j in range(4):
            pick[32 * r + j, j, :] = -1.0
    ones_pad = np.zeros((P, 64), f)
    ones_pad[:, 0:HD] = 1.0
    ones_pad[:, 48:48 + HD] = 1.0
    cst = np.concatenate([np.eye(P, dtype=f), (parity == 0).astype(f)[:, None], (parity == 1).astype(f)[:, None],
                          pick.reshape(P, -1), ones_pad], axis=1)
    arrays = {"xp": xp, "cp": cpad, "wc": wc, "wf": wf, "wi": wi, "brow": brow, "gates": gates, "cst": cst,
              "ldT": a["L1_ffn_lora_down"].T, "da": a["L1_ffn_down_aux"], "luT": a["L1_ffn_lora_up"].T,
              "uaT": a["L1_ffn_up_aux"].T}
    arrays = {k: np.ascontiguousarray(v) for k, v in arrays.items()}
    nc = bacc.Bacc("TRN2", target_bir_lowering=False, num_devices=1)
    aps = [nc.dram_tensor(k, v.shape, mybir.dt.from_np(v.dtype), kind="ExternalInput").ap() for k, v in arrays.items()]
    aps.append(nc.dram_tensor("y", (T, S, D), F32, kind="ExternalOutput").ap())
    flamingo_kernel(nc, *aps)
    r = run_bass_kernel_spmd(nc, [arrays], core_ids=[0])
    return r.results[0]["y"][STAGES_BEHIND:]
```

```python
from contextlib import ExitStack

import numpy as np

import concourse.bass as bass
from concourse import mybir


B, S, SC, D = 64, 256, 120, 256
H, HD = 16, 16
HID = 768
P = 128
KC = D // P
NT = S // P
HC = HID // P
HC_POOL = 4
INIT_POOL = 12
STAGES_BEHIND = 3
FRONT_X, FRONT_C = 1, 2
SLOT_Q = (0, 1, 2, 0, 1, 0)
SLOT_K = (0, 0, 0, 1, 1, 2)
SLOTS = len(SLOT_Q)
KS = SLOTS * HD
MAX_PARTS = 2
KM = KS + MAX_PARTS
GP = D // HD // KC
SCALE = float(np.float32(1.0 / 127.0))
EPS = 1e-5
SOFT = HD ** -0.5

F32 = mybir.dt.float32
F32R = mybir.dt.float32r
BF16 = mybir.dt.bfloat16
I32 = mybir.dt.int32
ALU = mybir.AluOpType
ACT = mybir.ActivationFunctionType
AX = mybir.AxisListType

SEG = {}
_at = 0
for _name, _cols in (("gate", KC * HID), ("up", KC * HID), ("down", HC * D),
                     ("q0", KC * D), ("q1", KC * D),
                     ("wo0", KC * D), ("wo1", KC * D), ("f1", KC * D)):
    SEG[_name] = _at
    _at += _cols
WCOLS = _at
CSEG = {"k0": 0, "v0": KC * D, "k1": 2 * KC * D, "v1": 2 * KC * D + KC * P}
CCOLS = 2 * KC * D + KC * P + KC * HD
ROUNDS = [("gate", KC * HID), ("up", KC * HID), ("down", HC * D), ("q0", 2 * KC * D), ("wo0", 2 * KC * D), ("f1", KC * D)]
STAGE = KC * HID
BIAS = {"q0": 0, "k0": D, "v0": 2 * D, "wo0": 3 * D, "f1": 4 * D}
NBIAS = 5 * D


def flamingo_kernel(nc, xp, cp, wc, wf, wi, brow, gates, cst, ldT, da, luT, uaT, out):
    iterations = out.shape[0]
    last_t = iterations
    ctx = ExitStack()
    with ctx:
        def sb(name, shape, dt=F32):
            return ctx.enter_context(nc.sbuf_tensor(name, shape, dt))

        def sem(name):
            return ctx.enter_context(nc.semaphore(name))

        w_hi = sb("w_hi", [P, WCOLS], F32R)
        w_lo = sb("w_lo", [P, WCOLS], F32R)
        ident = sb("ident", [P, P])
        masks = sb("masks", [P, 2])
        ones_pad = sb("ones_pad", [P, 64])
        neg_ident = sb("neg_ident", [P, P], F32R)
        w_ctx = sb("w_ctx", [P, CCOLS])
        ones_row = sb("ones_row", [1, P])
        bias_row = sb("bias_row", [1, 2 * D])
        ones2 = sb("ones2", [2, D], F32R)
        bias2 = sb("bias2", [2, NBIAS], F32R)
        minus_half = sb("minus_half", [P, NT])
        x_ln = sb("x_ln", [P, NT, D])
        x_res = sb("x_res", [P, NT, D])
        x1 = sb("x1", [P, NT, D])
        x2 = sb("x2", [P, NT, D])
        x2_before = sb("x2_before", [P, NT, D])
        x3 = sb("x3", [P, NT, D])
        y_out = sb("y_out", [P, NT, D])
        xn_AC, xn_BD = sb("xn_AC", [P, NT, D]), sb("xn_BD", [P, NT, D])
        xn = {"A": xn_AC, "B": xn_BD, "C": xn_AC, "D": xn_BD}
        xt_hi = {s: sb(f"xt_hi_{s}", [P, KC, S], F32R) for s in "ABCD"}
        xt_lo = {s: sb(f"xt_lo_{s}", [P, KC, S], F32R) for s in "ABCD"}
        stats = {s: sb(f"stats_{s}", [P, NT, 6]) for s in "ABCD"}
        mv = {s: sb(f"mv_{s}", [P, NT, 2]) for s in "ABCD"}
        var_eps = {s: sb(f"var_eps_{s}", [P, NT]) for s in "ABCD"}
        ln_count = sb("ln_count", [P, 1])
        neg_mean = {s: sb(f"neg_mean_{s}", [P, NT]) for s in "ABCD"}
        shift = {s: sb(f"shift_{s}", [P, NT]) for s in "ABCD"}
        rstd = {s: sb(f"rstd_{s}", [P, NT]) for s in "ABCD"}
        ctx_f = {s: sb(f"ctx_f_{s}", [P, KC, P]) for s in "AC"}
        q_rest = sb("q_rest", [P, KC * S])
        q_part = sb("q_part", [P, 3, KC * S], BF16)
        k0_rest = sb("k0_rest", [P, KC * P])
        k0_part = sb("k0_part", [P, 3, KC * P], BF16)
        qs = {s: sb(f"qs_{s}", [P, GP, KC * S], BF16) for s in "AC"}
        ks0 = sb("ks0", [P, GP, KC * P], BF16)
        ks1 = sb("ks1", [P, P], BF16)
        k1_first = sb("k1_first", [P, P], BF16)
        k1_rest = sb("k1_rest", [P, P])
        k1_second = sb("k1_second", [P, P], BF16)
        v0_pad = sb("v0_pad", [P, H // 2, 64])
        v1_pad = sb("v1_pad", [P, 64])
        m0 = sb("m0", [P, 2, P], F32R)
        m1 = sb("m1", [P, 2, H])
        m1_part = sb("m1_part", [H, MAX_PARTS, S], BF16)
        e0 = sb("e0", [P, NT, 4, 4, P])
        e1 = sb("e1", [P, KC, 4, 2, S])
        zt = sb("zt", [P, 8, P])
        z0 = sb("z0", [P, NT, P])
        rz0 = sb("rz0", [P, NT, P])
        y1f = sb("y1f", [P, KC * S])
        y_hi = {s: sb(f"y_hi_{s}", [P, KC, S], F32R) for s in "AC"}
        y_lo = {s: sb(f"y_lo_{s}", [P, KC, S], F32R) for s in "AC"}
        th = sb("th", [P, 2, S])
        act_g = sb("act_g", [P, 2, S])
        h_f = sb("h_f", [P, 2, S])
        h_hi = sb("h_hi", [P, HC, S], F32R)
        h_lo = sb("h_lo", [P, HC, S], F32R)
        e0_flat = e0[:, :, :, :, :].rearrange("p a b c d -> p (a b c d)")
        e1_flat = e1[:, :, :, :, :].rearrange("p a b c d -> p (a b c d)")
        stage = [e0_flat[:, 0:STAGE], e1_flat[:, 0:STAGE]]
        b_f = e1_flat[0:1, STAGE:STAGE + NBIAS]
        small = STAGE + NBIAS
        da_s = e1_flat[0:100, small:small + D]
        uaT_s = e1_flat[0:50, small + D:small + 2 * D]
        t1_s = e1_flat[0:4, small + 2 * D:small + 3 * D]
        t2_s = e1_flat[0:50, small + 3 * D:small + 4 * D]
        ldT_s = e1_flat[0:100, small + 4 * D:small + 4 * D + 4]
        luT_s = e1_flat[0:4, small + 4 * D + 4:small + 4 * D + 54]
        b_hi = h_hi[0:1, :, :].rearrange("p a b -> p (a b)")[:, 0:NBIAS]
        b_lo = h_lo[0:1, :, :].rearrange("p a b -> p (a b)")[:, 0:NBIAS]
        tg = sb("tg", [P, 4])
        graw = sb("graw", [P, 4])

        scores = ctx.enter_context(nc.psum_tensor("scores", [P, 4, 512], F32))
        W = [ctx.enter_context(nc.psum_tensor(f"work{i}", [P, 512], F32)) for i in range(4)]

        names = []
        names += ["ld_cst", "ld_w0", "ld_w1", "w_scaled", "w_hi", "w_lo", "tg", "b_scaled", "b_split", "ld_bias2",
                  "li_t1", "li_t1s", "li_t2", "li_t2s", "li", "cst_r", "dequantised", "init_dve", "init_pool"]
        names += ["ld_ctx_C", "ld_ctx_A", "ld_x_ln", "ld_x_res", "st_out"]
        names += [f"{p}_{s}" for p in ("ln_mom", "ln_eps", "ln_rstd", "ln", "T_mm", "T_hi", "T_lo")
                  for s in "ABCD"]
        names += ["kv1_mm", "k1_first", "k1_rest", "k1_second", "ks1", "v1_pad",
                  "k0_mm", "k0_p1", "k0_rest", "k0_p2", "k0_p3", "v0_mm", "v0_pad"]
        names += [f"q_{p}_{s}" for p in ("mm", "p1", "rest", "p2", "p3") for s in "AC"]
        names += ["M0_mm", "M1_mm", "M0_max", "M1_max", "mT_mm", "m_p1", "m_p2"]
        names += ["T0_mm", "T1_mm"]
        names += [f"A{c}_{p}" for c in (0, 1) for p in ("mm", "max", "z", "rz", "p")]
        names += ["yA_mm", "yA_hi", "yA_lo", "woA_mm", "res_A"]
        names += ["yC_mm", "zC_mm", "zC", "rzC", "yC", "yC_hi", "yC_lo", "woC_mm", "res_C"]
        names += ["dn_mm", "res_B", "x2_before", "f1_mm", "res_D"]
        hidden = [f"G_{p}" for p in ("mm", "tanh", "a", "h", "hi", "lo")]
        names += hidden + ["G_lo_last"]
        exponentials = ["T0_exp", "T1_exp", "A0_exp", "A1_exp", "A0_sub", "A1_sub"]
        names += exponentials
        names += ["ld_k0", "ld_q_A", "ld_q_C", "ld_m", "z_part", "ln_root"]
        stacking = {"ld_k0": 16 * SLOTS, "ld_q_A": 16 * SLOTS, "ld_q_C": 16 * SLOTS, "ld_m": 16 * MAX_PARTS}
        s = {n: sem(n) for n in names}
        unprimed = names[:names.index("T_mm_A")] + names[names.index("ld_k0"):]
        primed = ["st_out"] + [n for n in names if n.startswith("ln_") and not n.startswith(("ln_mom", "ln_root"))]
        primed += [n for n in names if n not in unprimed]

        def chunk(m, t):
            return t * HC + (m + 1 - HC)

        def chunk_lo(m, t):
            return t * HC_POOL + (m + 1 - HC_POOL)

        def half(h, t):
            return t * 2 + (h - 1)

        def w(which, name, off, n):
            a = SEG[name] + off
            return (w_hi if which == "hi" else w_lo)[:, a:a + n]

        block = ctx.enter_context(nc.Block())

        @block.sync
        def _(sp):
            sp.dma_start(ident[:, :], cst[:, 0:P]).then_inc(s["ld_cst"], 16)
            sp.dma_start(masks[:, :], cst[:, P:P + 2]).then_inc(s["ld_cst"], 16)
            sp.dma_start(ones_pad[:, :], cst[:, P + 2:P + 66]).then_inc(s["ld_cst"], 16)
            sp.dma_start(w_ctx[:, :], wc).then_inc(s["ld_cst"], 16)
            sp.dma_start(bias_row[:, :], brow[:, BIAS["k0"]:BIAS["k0"] + 2 * D]).then_inc(s["ld_cst"], 16)
            sp.dma_start(graw[:, :], gates).then_inc(s["ld_cst"], 16)
            sp.dma_start(b_f[:, :], brow).then_inc(s["ld_cst"], 16)
            sp.dma_start(ldT_s[:, :], ldT).then_inc(s["ld_cst"], 16)
            sp.dma_start(da_s[:, :], da).then_inc(s["ld_cst"], 16)
            sp.dma_start(luT_s[:, :], luT).then_inc(s["ld_cst"], 16)
            sp.dma_start(uaT_s[:, :], uaT).then_inc(s["ld_cst"], 16)
            for r, (name, n) in enumerate(ROUNDS):
                if r >= 2:
                    sp.wait_ge(s["w_lo"], r - 1)
                src = wi[:, SEG[name]:SEG[name] + n] if r < 3 else wf[:, SEG[name] - SEG["q0"]:SEG[name] - SEG["q0"] + n]
                dst = stage[r % 2][:, 0:n]
                sp.dma_start(dst.bitcast(I32) if r < 3 else dst, src).then_inc(s[f"ld_w{r % 2}"], 16)
            sp.wait_ge(s["b_split"], 2)
            sp.dma_start(bias2[0:1, :].bitcast(F32), b_hi.bitcast(F32)).then_inc(s["ld_bias2"], 16)
            sp.dma_start(bias2[1:2, :].bitcast(F32), b_lo.bitcast(F32)).then_inc(s["ld_bias2"], 16)
            for n, count in stacking.items():
                sp.sem_inc(s[n], count)
            for n in primed:
                sp.sem_inc(s[n], 16 if n == "st_out" else HC_POOL if n == "G_lo" else HC if n in hidden else 2 if n in exponentials else 1)

            def stack(dst, src, part, slots, name):
                for slot, p in enumerate(slots):
                    if p == part:
                        sp.dma_start(dst[slot * HD:(slot + 1) * HD, :, :],
                                     src[:, part, :]).then_inc(s[name], 16)

            def load_x_ln(t):
                sp.dma_start(x_ln[:, :, :], xp[t - 1, :, :].rearrange("(i p) d -> p i d", p=P)).then_inc(s["ld_x_ln"], 16)

            def load_x_res(t):
                sp.dma_start(x_res[:, :, :], xp[t - 2, :, :].rearrange("(i p) d -> p i d", p=P)).then_inc(s["ld_x_res"], 16)

            def load_ctx(st, t):
                sp.dma_start(ctx_f[st][:, :, :], cp[t - 2 if st == "C" else t, :, :, :]).then_inc(s[f"ld_ctx_{st}"], 16)

            load_ctx("A", 2)
            load_x_ln(2)
            load_ctx("C", 2)
            load_x_res(2)
            with nc.sync.Fori(2, last_t + 2) as t:
                sp.wait_ge(s["A1_mm"], t - 1)
                sp.wait_ge(s["k0_p1"], t)
                stack(ks0, k0_part, 0, SLOT_K, "ld_k0")
                sp.wait_ge(s["k0_p2"], t)
                stack(ks0, k0_part, 1, SLOT_K, "ld_k0")
                sp.wait_ge(s["k0_p3"], t)
                stack(ks0, k0_part, 2, SLOT_K, "ld_k0")
                sp.wait_ge(s["T1_mm"], t)
                for part in range(3):
                    sp.wait_ge(s[f"q_p{part + 1}_C"], t)
                    stack(qs["C"], q_part, part, SLOT_Q, "ld_q_C")
                sp.wait_ge(s["ln_A"], t)
                load_x_ln(t + 1)
                sp.wait_ge(s["kv1_mm"], t)
                load_ctx("C", t + 1)
                sp.wait_ge(s["A1_mm"], t - 1)
                for part in range(3):
                    sp.wait_ge(s[f"q_p{part + 1}_A"], t)
                    stack(qs["A"], q_part, part, SLOT_Q, "ld_q_A")
                sp.wait_ge(s["res_A"], t)
                load_x_res(t + 1)
                for part in range(MAX_PARTS):
                    sp.wait_ge(s[f"m_p{part + 1}"], t)
                    sp.dma_start(qs["C"][KS + part:KS + part + 1, :, :].rearrange("p h (k n) -> p (h k) n", k=KC),
                                 m1_part[:, part, :]).then_inc(s["ld_m"], 16)
                sp.wait_ge(s["v0_mm"], t)
                load_ctx("A", t + 1)
                sp.wait_ge(s["res_D"], t)
                sp.dma_start(out[t - 2, :, :].rearrange("(i p) d -> p i d", p=P), y_out[:, :, :]).then_inc(s["st_out"], 16)
            sp.wait_ge(s["st_out"], 16 * (last_t + 1))

        @block.gpsimd
        def _(pool):
            pool.memset(minus_half[:, :], -0.5).then_inc(s["init_pool"], 1)
            pool.memset(v0_pad[:, :, :], 0.0).then_inc(s["init_pool"], 1)
            pool.memset(v1_pad[:, :], 0.0).then_inc(s["init_pool"], 1)
            pool.memset(ones2[:, :].bitcast(F32), 1.0).then_inc(s["init_pool"], 1)
            pool.memset(ones_row[:, :], 1.0).then_inc(s["init_pool"], 1)
            pool.memset(ks1[:, :], 1.0).then_inc(s["init_pool"], 1)
            for tile in (x2, x2_before, xn["C"], qs["C"]):
                pool.memset(tile[:, :, :], 0.0).then_inc(s["init_pool"], 1)
            pool.memset(z0[:, 1, :], 1.0).then_inc(s["init_pool"], 1)
            pool.wait_ge(s["w_lo"], len(ROUNDS) - 1)
            pool.memset(e0[:, :, :, :, :], 0.0).then_inc(s["init_pool"], 1)
            pool.wait_ge(s["init_pool"], INIT_POOL)

            def root(st, k, t):
                pool.wait_ge(s[f"ln_eps_{st}"], t)
                pool.wait_ge(s[f"ln_{st}"], t - 1)
                pool.tensor_tensor(rstd[st][:, :], var_eps[st][:, :], minus_half[:, :], ALU.pow)\
                    .then_inc(s["ln_root"], 1)
                pool.wait_ge(s["ln_root"], 4 * (t - 2) + (k + 1))
                pool.tensor_tensor(shift[st][:, :], neg_mean[st][:, :], rstd[st][:, :], ALU.mult)\
                    .then_inc(s[f"ln_rstd_{st}"], 1)

            def hidden_lo(m, t):
                pool.wait_ge(s["G_hi"], chunk(m, t))
                pool.tensor_tensor(h_lo[:, m, :], h_f[:, m % 2, :], h_hi[:, m, :].bitcast(F32), ALU.subtract)\
                    .then_inc(s["G_lo"], 1)

            def third(st, t):
                pool.wait_ge(s[f"q_p2_{st}"], t)
                pool.tensor_tensor(q_part[:, 2, :], q_rest[:, :], q_part[:, 1, :], ALU.subtract)\
                    .then_inc(s[f"q_p3_{st}"], 1)

            def sum_heads(c, t):
                if c == 1:
                    pool.wait_ge(s["A0_z"], t)
                else:
                    pool.wait_ge(s["A1_z"], t - 1)
                for h in range(2):
                    if (c, h) == (1, 1):
                        root("C", 3, t)
                    pool.wait_ge(s[f"A{c}_exp"], half(h, t))
                    last = pool.tensor_tensor(zt[0:SC, 4 * h:4 * h + 4, :], e0[0:SC, c, 2 * h, :, :],
                                              e0[0:SC, c, 2 * h + 1, :, :], ALU.add)
                last.then_inc(s["z_part"], 1)
                pool.wait_ge(s["z_part"], 6 * (t - 2) + 3 * c + 1)
                pool.tensor_tensor(zt[0:SC, 0:4, :], zt[0:SC, 0:4, :], zt[0:SC, 4:8, :], ALU.add)\
                    .then_inc(s["z_part"], 1)
                pool.wait_ge(s["z_part"], 6 * (t - 2) + 3 * c + 2)
                pool.tensor_tensor(zt[0:SC, 0:2, :], zt[0:SC, 0:2, :], zt[0:SC, 2:4, :], ALU.add)\
                    .then_inc(s["z_part"], 1)
                pool.wait_ge(s["z_part"], 6 * (t - 2) + 3 * c + 3)
                pool.tensor_tensor(z0[0:SC, c, :], zt[0:SC, 0, :], zt[0:SC, 1, :], ALU.add).then_inc(s[f"A{c}_z"], 1)

            with nc.gpsimd.Fori(2, last_t + 2) as t:
                root("A", 0, t)
                pool.wait_ge(s["k0_p2"], t)
                pool.tensor_tensor(k0_part[:, 2, :], k0_rest[:, :], k0_part[:, 1, :], ALU.subtract)\
                    .then_inc(s["k0_p3"], 1)
                third("C", t)
                root("B", 1, t)
                third("A", t)
                root("D", 2, t)
                for m in range(HC_POOL):
                    hidden_lo(m, t)
                sum_heads(0, t)
                sum_heads(1, t)

        @block.scalar
        def _(act):
            act.wait_ge(s["ld_cst"], 16 * 11)
            act.activation(tg[:, :], graw[:, :], ACT.Tanh).then_inc(s["tg"], 1)
            act.activation(neg_ident[:, :], ident[:, :], ACT.Copy, scale=-1.0).then_inc(s["cst_r"], 1)
            act.wait_ge(s["b_scaled"], 2)
            act.activation(b_hi[:, :], b_f[:, :], ACT.Copy).then_inc(s["b_split"], 1)
            for r, (name, n) in enumerate(ROUNDS):
                act.wait_ge(s["w_scaled"], r + 1)
                act.activation(w_hi[:, SEG[name]:SEG[name] + n], stage[r % 2][:, 0:n], ACT.Copy).then_inc(s["w_hi"], 1)
            act.wait_ge(s["init_pool"], INIT_POOL)
            act.wait_ge(s["init_dve"], 1)

            def split_hi(out, src, name):
                return act.activation(out, src, ACT.Copy).then_inc(s[name], 1)

            def transposed_hi(st, bank, readers, t):
                act.wait_ge(s[f"T_mm_{st}"], t)
                act.wait_ge(s[readers], t - 1)
                split_hi(xt_hi[st][:, :, :], W[bank][:, :].rearrange("p (k n) -> p k n", k=KC), f"T_hi_{st}")

            def ln_apply(st, x, t):
                act.wait_ge(s[f"ln_rstd_{st}"], t)
                for i in range(NT):
                    last = act.activation(xn[st][:, i, :], x[:, i, :], ACT.Identity, bias=shift[st][:, i:i + 1],
                                          scale=rstd[st][:, i:i + 1])
                last.then_inc(s[f"ln_{st}"], 1)

            def query_parts(st, bank, t):
                act.wait_ge(s[f"q_mm_{st}"], t)
                if st == "A":
                    act.wait_ge(s["ld_q_C"], 16 * SLOTS * t)
                else:
                    act.wait_ge(s["ld_q_A"], 16 * SLOTS * (t - 1))
                split_hi(q_part[:, 0, :], W[bank][:, :], f"q_p1_{st}")
                act.wait_ge(s[f"q_rest_{st}"], t)
                split_hi(q_part[:, 1, :], q_rest[:, :], f"q_p2_{st}")

            def tanh(m, bank, t):
                act.wait_ge(s["G_mm"], chunk(m, t))
                act.wait_ge(s["G_a"], chunk(m - 2, t))
                act.activation(th[:, m % 2, :], W[bank][:, 0:S], ACT.Tanh, scale=0.5).then_inc(s["G_tanh"], 1)

            def hidden_hi(m, t):
                act.wait_ge(s["G_h"], chunk(m, t))
                act.wait_ge(s["dn_mm"], t - 1)
                split_hi(h_hi[:, m, :], h_f[:, m % 2, :], "G_hi")

            def exps(e, c, name, halves=(0, 1), subtracted=None, t=None):
                for h in halves:
                    if subtracted:
                        act.wait_ge(s[subtracted], half(h, t))
                    act.activation(e[0:SC, c, 2 * h:2 * h + 2, :, :].rearrange("p a b n -> p (a b n)"),
                                   scores[0:SC, 2 * h:2 * h + 2, :].rearrange("p a n -> p (a n)"),
                                   ACT.Exp, scale=SOFT).then_inc(s[f"{name}_exp"], 1)

            with nc.scalar.Fori(2, last_t + 2) as t:
                act.wait_ge(s["k0_mm"], t)
                act.wait_ge(s["ld_k0"], 16 * SLOTS * (t - 1))
                split_hi(k0_part[:, 0, :], W[2][:, 0:KC * P], "k0_p1")
                transposed_hi("C", 3, "q_mm_C", t)
                act.wait_ge(s["T1_mm"], t)
                exps(e1, 1, "T1")
                ln_apply("A", x_ln, t)
                act.wait_ge(s["zC_mm"], t)
                act.wait_ge(s["yC_lo"], t - 1)
                act.activation(y1f[:, :], W[1][:, :], ACT.Copy).then_inc(s["zC"], 1)
                act.wait_ge(s["k0_rest"], t)
                split_hi(k0_part[:, 1, :], k0_rest[:, :], "k0_p2")
                act.wait_ge(s["q_mm_C"], t)
                act.wait_ge(s["ld_q_A"], 16 * SLOTS * (t - 1))
                split_hi(q_part[:, 0, :], W[3][:, :], "q_p1_C")
                transposed_hi("A", 1, "q_mm_A", t)
                act.wait_ge(s["q_rest_C"], t)
                split_hi(q_part[:, 1, :], q_rest[:, :], "q_p2_C")
                act.wait_ge(s["yA_mm"], t)
                act.wait_ge(s["woA_mm"], t - 1)
                split_hi(y_hi["A"][:, :, :], W[2][:, :].rearrange("p (k n) -> p k n", k=KC), "yA_hi")
                act.wait_ge(s["kv1_mm"], t)
                split_hi(k1_first[:, :], W[3][:, 0:P], "k1_first")
                act.activation(v1_pad[0:SC, 0:HD], W[3][0:SC, P:P + HD], ACT.Copy)
                act.activation(v1_pad[0:SC, 48:48 + HD], W[3][0:SC, P:P + HD], ACT.Copy).then_inc(s["v1_pad"], 1)
                act.wait_ge(s["yC"], t)
                act.wait_ge(s["woC_mm"], t - 1)
                split_hi(y_hi["C"][:, :, :], y1f[:, :].rearrange("p (k n) -> p k n", k=KC), "yC_hi")
                act.wait_ge(s["q_mm_A"], t)
                act.wait_ge(s["ld_q_C"], 16 * SLOTS * t)
                split_hi(q_part[:, 0, :], W[1][:, :], "q_p1_A")
                act.wait_ge(s["v0_mm"], t)
                v_src = W[2][0:SC, 0:D].rearrange("p (g r j) -> p g r j", r=2, j=HD)
                act.activation(v0_pad[0:SC, :, 0:HD], v_src[:, :, 0, :], ACT.Copy)
                act.activation(v0_pad[0:SC, :, 48:48 + HD], v_src[:, :, 1, :], ACT.Copy).then_inc(s["v0_pad"], 1)
                ln_apply("B", x1, t)
                act.wait_ge(s["q_rest_A"], t)
                split_hi(q_part[:, 1, :], q_rest[:, :], "q_p2_A")
                transposed_hi("B", 2, "dn_mm", t)
                act.wait_ge(s["res_C"], t)
                act.activation(x2_before[:, :, :], x2[:, :, :], ACT.Copy).then_inc(s["x2_before"], 1)
                tanh(0, 3, t)
                tanh(1, 2, t)
                ln_apply("D", x3, t)
                hidden_hi(0, t)
                hidden_hi(1, t)
                tanh(2, 1, t)
                transposed_hi("D", 2, "f1_mm", t)
                tanh(3, 3, t)
                hidden_hi(2, t)
                act.wait_ge(s["mT_mm"], t)
                act.wait_ge(s["ld_m"], 16 * MAX_PARTS * (t - 1))
                act.activation(m1_part[:, 0, :], W[0][0:H, 0:S], ACT.Copy, scale=-1.0).then_inc(s["m_p1"], 1)
                tanh(4, 1, t)
                hidden_hi(3, t)
                tanh(5, 3, t)
                exps(e0, 0, "A0", subtracted="A0_sub", t=t)
                hidden_hi(4, t)
                hidden_hi(5, t)
                exps(e0, 1, "A1", subtracted="A1_sub", t=t)
                act.wait_ge(s["T0_mm"], t)
                exps(e1, 0, "T0", (0,))
                ln_apply("C", x2, t)
                exps(e1, 0, "T0", (1,))

        @block.vector
        def _(dve):
            dve.wait_ge(s["tg"], 1)
            dve.tensor_scalar(b_f[:, BIAS["wo0"]:BIAS["wo0"] + D], b_f[:, BIAS["wo0"]:BIAS["wo0"] + D],
                              tg[0:1, 0:1], None, ALU.mult).then_inc(s["b_scaled"], 1)
            dve.tensor_scalar(b_f[:, BIAS["f1"]:BIAS["f1"] + D], b_f[:, BIAS["f1"]:BIAS["f1"] + D],
                              tg[0:1, 3:4], None, ALU.mult).then_inc(s["b_scaled"], 1)
            dve.wait_ge(s["b_split"], 1)
            dve.tensor_tensor(b_lo[:, :], b_f[:, :], b_hi[:, :].bitcast(F32), ALU.subtract).then_inc(s["b_split"], 1)
            for r, (name, n) in enumerate(ROUNDS):
                st = stage[r % 2][:, 0:n]
                dve.wait_ge(s[f"ld_w{r % 2}"], 16 * (r // 2 + 1))
                if name in ("gate", "up"):
                    dve.tensor_scalar(st, st.bitcast(I32), SCALE, None, ALU.mult).then_inc(s["w_scaled"], 1)
                elif name == "down":
                    dve.tensor_scalar(st, st.bitcast(I32), SCALE, None, ALU.mult).then_inc(s["dequantised"], 1)
                    dve.wait_ge(s["dequantised"], 1)
                    dve.tensor_scalar(st, st, tg[:, 2:3], 0.5, ALU.mult, ALU.mult).then_inc(s["w_scaled"], 1)
                elif name == "wo0":
                    dve.tensor_scalar(st[:, 0:KC * D], st[:, 0:KC * D], tg[:, 0:1], None, ALU.mult)
                    dve.tensor_scalar(st[:, KC * D:], st[:, KC * D:], tg[:, 1:2], None, ALU.mult)\
                        .then_inc(s["w_scaled"], 1)
                elif name == "f1":
                    dve.wait_ge(s["li_t1"], 1)
                    dve.tensor_copy(t1_s[:, :], W[0][0:4, 0:D]).then_inc(s["li_t1s"], 1)
                    dve.wait_ge(s["li_t2"], 1)
                    dve.tensor_copy(t2_s[:, :], W[1][0:50, 0:D]).then_inc(s["li_t2s"], 1)
                    dve.wait_ge(s["li"], 1)
                    dve.tensor_tensor(st, W[2][:, :], st, ALU.add).then_inc(s["li_t2s"], 1)
                    dve.wait_ge(s["li_t2s"], 2)
                    dve.tensor_scalar(st, st, tg[:, 3:4], None, ALU.mult).then_inc(s["w_scaled"], 1)
                else:
                    dve.engine_nop().then_inc(s["w_scaled"], 1)
                dve.wait_ge(s["w_hi"], r + 1)
                dve.tensor_tensor(w_lo[:, SEG[name]:SEG[name] + n], st, w_hi[:, SEG[name]:SEG[name] + n].bitcast(F32),
                                  ALU.subtract).then_inc(s["w_lo"], 1)
            dve.wait_ge(s["w_lo"], len(ROUNDS))
            dve.memset(e1[:, :, :, :, :], 1.0).then_inc(s["init_dve"], 1)
            dve.wait_ge(s["init_pool"], INIT_POOL)

            def ln_stats(st, x, t):
                for i in range(NT):
                    last = dve.bn_stats(stats[st][:, i, :], x[:, i, :])
                last.then_inc(s[f"ln_mom_{st}"], 1)
                dve.wait_ge(s[f"ln_mom_{st}"], 2 * t - 3)
                dve.tensor_copy(ln_count[:, :], stats[st][:, 0, 0:1])
                for i in range(NT):
                    last = dve.bn_aggr(mv[st][:, i, :], stats[st][:, i, :])
                last.then_inc(s[f"ln_mom_{st}"], 1)
                dve.wait_ge(s[f"ln_mom_{st}"], 2 * t - 2)
                dve.wait_ge(s[f"ln_rstd_{st}"], t - 1)
                dve.tensor_scalar(neg_mean[st][:, :], mv[st][:, :, 0], -1.0, None, ALU.mult)
                dve.tensor_scalar(var_eps[st][:, :], mv[st][:, :, 1], EPS, None, ALU.add).then_inc(s[f"ln_eps_{st}"], 1)

            def low(out, src, hi, name):
                return dve.tensor_tensor(out, src, hi.bitcast(F32), ALU.subtract).then_inc(s[name], 1)

            def transposed_lo(st, bank, t):
                dve.wait_ge(s[f"T_hi_{st}"], t)
                low(xt_lo[st][:, :, :], W[bank][:, :].rearrange("p (k n) -> p k n", k=KC), xt_hi[st][:, :, :],
                    f"T_lo_{st}")

            def gated(m, bank, t):
                dve.wait_ge(s["G_tanh"], chunk(m, t))
                dve.scalar_tensor_tensor(act_g[:, m % 2, :], th[:, m % 2, :], 1.0, W[bank][:, 0:S],
                                         ALU.add, ALU.mult).then_inc(s["G_a"], 1)
                dve.wait_ge(s["G_a"], chunk(m, t))
                if m >= 2:
                    dve.wait_ge(s["G_lo"], chunk_lo(m - 2, t))
                else:
                    dve.wait_ge(s["G_lo_last"], t - 1)
                dve.tensor_tensor(h_f[:, m % 2, :], W[bank][:, S:2 * S], act_g[:, m % 2, :], ALU.mult)\
                    .then_inc(s["G_h"], 1)

            def hidden_lo(m, t):
                dve.wait_ge(s["G_hi"], chunk(m, t))
                last = dve.tensor_tensor(h_lo[:, m, :], h_f[:, m % 2, :], h_hi[:, m, :].bitcast(F32), ALU.subtract)
                if m == HC - 1:
                    last.then_inc(s["G_lo_last"], 1)

            def head_max(c, t):
                dve.wait_ge(s[f"A{c}_mm"], t)
                dve.tensor_reduce(m0[0:SC, c, :], scores[0:SC, :, :].rearrange("p r (h n) -> p n (r h)", n=P),
                                  AX.X, ALU.max).then_inc(s[f"A{c}_max"], 1)

            def key_max(c, t):
                dve.wait_ge(s[f"M{c}_mm"], t)
                dve.wait_ge(s["mT_mm"], t - 1)
                dve.tensor_reduce(m1[:, c, :].rearrange("p (r j) -> p r j", r=4),
                                  scores[:, :, :].rearrange("p r (h n) -> p r h n", n=P)[:, :, :, 0:SC],
                                  AX.X, ALU.max).then_inc(s[f"M{c}_max"], 1)

            def normalise(c, t, when):
                dve.wait_ge(s[f"A{c}_z"], when)
                dve.reciprocal(rz0[0:SC, c, :], z0[0:SC, c, :]).then_inc(s[f"A{c}_rz"], 1)
                dve.wait_ge(s[f"A{c}_rz"], t)
                e = e0[0:SC, c, :, :, :].rearrange("p a b n -> p (a b) n")
                dve.tensor_tensor(e, e, rz0[0:SC, c:c + 1, :].to_broadcast([SC, H, P]), ALU.mult)\
                    .then_inc(s[f"A{c}_p"], 1)

            def residual(out, x, bank, mm, name, t):
                dve.wait_ge(s[mm], t)
                dve.tensor_tensor(out[:, :, :], W[bank][:, :].rearrange("p (i d) -> p i d", i=NT), x[:, :, :], ALU.add)\
                    .then_inc(s[name], 1)
                dve.wait_ge(s[name], t)

            def query_rest(st, bank, t):
                dve.wait_ge(s[f"q_p1_{st}"], t)
                dve.wait_ge(s["q_p3_C"], t if st == "A" else t - 1)
                dve.wait_ge(s["q_p3_A"], t - 1)
                dve.tensor_tensor(q_rest[:, :], W[bank][:, :], q_part[:, 0, :], ALU.subtract)\
                    .then_inc(s[f"q_rest_{st}"], 1)

            with nc.vector.Fori(2, last_t + 2) as t:
                dve.wait_ge(s["ld_x_ln"], 16 * (t - 1))
                ln_stats("A", x_ln, t)
                dve.wait_ge(s["k0_p1"], t)
                dve.wait_ge(s["k0_p3"], t - 1)
                dve.tensor_tensor(k0_rest[:, :], W[2][:, 0:KC * P], k0_part[:, 0, :], ALU.subtract)\
                    .then_inc(s["k0_rest"], 1)
                transposed_lo("C", 3, t)
                normalise(1, t, t - 1)
                dve.wait_ge(s["zC"], t)
                dve.reciprocal(y1f[:, 0:S], y1f[:, 0:S])
                query_rest("C", 3, t)
                transposed_lo("A", 1, t)
                dve.reciprocal(y1f[:, S:S + P], y1f[:, S:S + P])
                dve.wait_ge(s["yA_hi"], t)
                low(y_lo["A"][:, :, :], W[2][:, :].rearrange("p (k n) -> p k n", k=KC), y_hi["A"][:, :, :], "yA_lo")
                dve.reciprocal(y1f[:, S + P:], y1f[:, S + P:]).then_inc(s["rzC"], 1)
                dve.wait_ge(s["k1_first"], t)
                dve.wait_ge(s["v1_pad"], t)
                dve.scalar_tensor_tensor(k1_rest[:, :], k1_first[:, :], masks[:, 0:1], W[3][:, 0:P],
                                         ALU.mult, ALU.add).then_inc(s["k1_rest"], 1)
                dve.wait_ge(s["rzC"], t)
                dve.wait_ge(s["yC_mm"], t)
                dve.tensor_tensor(y1f[:, :], W[0][:, :], y1f[:, :], ALU.mult).then_inc(s["yC"], 1)
                dve.wait_ge(s["ld_x_res"], 16 * (t - 1))
                residual(x1, x_res, 2, "woA_mm", "res_A", t)
                ln_stats("B", x1, t)
                dve.wait_ge(s["yC_hi"], t)
                low(y_lo["C"][:, :, :], y1f[:, :].rearrange("p (k n) -> p k n", k=KC), y_hi["C"][:, :, :], "yC_lo")
                dve.wait_ge(s["k1_rest"], t)
                dve.tensor_copy(k1_second[:, :], k1_rest[:, :]).then_inc(s["k1_second"], 1)
                dve.wait_ge(s["k1_second"], t)
                dve.wait_ge(s["T1_mm"], t)
                dve.scalar_tensor_tensor(ks1[0:KS, :], k1_second[0:KS, :], masks[0:KS, 1:2], k1_rest[0:KS, :],
                                         ALU.mult, ALU.add).then_inc(s["ks1"], 1)
                query_rest("A", 1, t)
                residual(x3, x2_before, 0, "woC_mm", "res_C", t)
                transposed_lo("B", 2, t)
                key_max(0, t)
                ln_stats("D", x3, t)
                gated(0, 3, t)
                gated(1, 2, t)
                key_max(1, t)
                gated(2, 1, t)
                gated(3, 3, t)
                head_max(0, t)
                transposed_lo("D", 2, t)
                dve.wait_ge(s["m_p1"], t)
                dve.scalar_tensor_tensor(m1_part[:, 1, :], W[0][0:H, 0:S], -1.0, m1_part[:, 0, :],
                                         ALU.mult, ALU.subtract).then_inc(s["m_p2"], 1)
                gated(4, 1, t)
                gated(5, 3, t)
                hidden_lo(4, t)
                hidden_lo(5, t)
                head_max(1, t)
                dve.wait_ge(s["x2_before"], t)
                residual(x2, x1, 1, "dn_mm", "res_B", t)
                ln_stats("C", x2, t)
                dve.wait_ge(s["st_out"], 16 * (t - 1))
                residual(y_out, x3, 0, "f1_mm", "res_D", t)
                normalise(0, t, t)

        @block.tensor
        def _(pe):
            pe.wait_ge(s["ld_cst"], 16 * 11)
            pe.matmul(W[0][0:4, 0:D], ldT_s[:, :], da_s[:, :], start=True, stop=True).then_inc(s["li_t1"], 1)
            pe.wait_ge(s["li_t1s"], 1)
            pe.matmul(W[1][0:50, 0:D], luT_s[:, :], t1_s[:, :], start=True, stop=True).then_inc(s["li_t2"], 1)
            pe.wait_ge(s["li_t2s"], 1)
            for kc in range(KC):
                last = pe.matmul(W[2][:, kc * D:(kc + 1) * D], t2_s[:, kc * P:(kc + 1) * P], uaT_s[:, :],
                                 start=True, stop=True)
            last.then_inc(s["li"], 1)
            pe.wait_ge(s["w_lo"], len(ROUNDS))
            pe.wait_ge(s["ld_bias2"], 32)
            pe.wait_ge(s["cst_r"], 1)
            pe.wait_ge(s["init_pool"], INIT_POOL)
            pe.wait_ge(s["init_dve"], 1)

            def product(out, terms, bias=None):
                first = True
                for n, ((a_hi, a_lo), (b_hi_, b_lo_)) in enumerate(terms):
                    end = n == len(terms) - 1 and bias is None
                    pe.matmul(out, a_hi, b_hi_, start=first, stop=False)
                    pe.matmul(out, a_hi, b_lo_, start=False, stop=False)
                    last = pe.matmul(out, a_lo, b_hi_, start=False, stop=end)
                    first = False
                if bias is not None:
                    last = pe.matmul(out, bias[0], bias[1], start=False, stop=True)
                return last

            def pair(hi, lo, *index):
                return hi[index], lo[index]

            def wpair(name, off, n):
                return w("hi", name, off, n), w("lo", name, off, n)

            def wc_of(name, off, n):
                return w_ctx[:, CSEG[name] + off:CSEG[name] + off + n]

            def transposes(st, bank):
                for i in range(NT):
                    for kc in range(KC):
                        last = pe.transpose(W[bank][:, kc * S + i * P:kc * S + (i + 1) * P],
                                            xn[st][:, i, kc * P:(kc + 1) * P], ident[:, :])
                return last.then_inc(s[f"T_mm_{st}"], 1)

            def queries(st, bank, name, bias):
                for oc in range(KC):
                    last = product(W[bank][:, oc * S:(oc + 1) * S],
                                   [(wpair(name, kc * D + oc * P, P), (xt_hi[st][:, kc, :], xt_lo[st][:, kc, :]))
                                    for kc in range(KC)],
                                   (bias2[:, BIAS[name] + oc * P:BIAS[name] + (oc + 1) * P], ones2[:, 0:S])
                                   if bias else None)
                return last.then_inc(s[f"q_mm_{st}"], 1)

            def rows_out(bank, a_hi, a_lo, name, chunks, bias=False):
                for i in range(NT):
                    last = product(W[bank][:, i * D:(i + 1) * D],
                                   [((a_hi[:, kc, i * P:(i + 1) * P], a_lo[:, kc, i * P:(i + 1) * P]),
                                     wpair(name, kc * D, D)) for kc in range(chunks)],
                                   (ones2[:, 0:P], bias2[:, BIAS[name]:BIAS[name] + D]) if bias else None)
                return last

            def gate_up(m, bank, t):
                for half, name in ((0, "gate"), (1, "up")):
                    last = product(W[bank][:, half * S:(half + 1) * S],
                                   [(wpair(name, kc * HID + m * P, P), (xt_hi["B"][:, kc, :], xt_lo["B"][:, kc, :]))
                                    for kc in range(KC)])
                last.then_inc(s["G_mm"], 1)

            def key_scores(c):
                for h in range(GP):
                    for cc in range(KC):
                        j = 2 * (h % 2) + cc
                        last = pe.matmul(scores[:, h // 2, j * P:(j + 1) * P],
                                         qs["C"][0:KS, h, cc * S + c * P:cc * S + (c + 1) * P], ks1[0:KS, :],
                                         start=True, stop=True)
                last.then_inc(s[f"M{c}_mm"], 1)

            def scores0(c, t):
                for h in range(GP):
                    if c == 1 and h % 4 == 0:
                        pe.wait_ge(s["A0_exp"], half(h // 4, t))
                    for cc in range(KC):
                        j = 2 * cc + h % 2
                        last = pe.matmul(scores[:, h // 2, j * P:(j + 1) * P], ks0[0:KS, h, cc * P:(cc + 1) * P],
                                         qs["A"][0:KS, h, cc * S + c * P:cc * S + (c + 1) * P],
                                         start=h % 2 == 0 and cc == 0, stop=False, skip_group_check=True)
                last.then_inc(s[f"A{c}_mm"], 1)

            def scores1(cc, before, t):
                for r in range(4):
                    if r % 2 == 0:
                        pe.wait_ge(s[f"{before}_exp"], half(r // 2, t))
                    last = pe.matmul(scores[:, r, :].rearrange("p (a n) -> p a n", a=2), ks1[0:KM, :],
                                     qs["C"][0:KM, 2 * r:2 * r + 2, cc * S:(cc + 1) * S],
                                     start=True, stop=True)
                last.then_inc(s[f"T{cc}_mm"], 1)

            def subtract_max(c, t):
                pe.wait_ge(s[f"A{c}_max"], t)
                for r in range(4):
                    last = pe.matmul(scores[:, r, :].rearrange("p (h n) -> p h n", n=P), neg_ident[0:SC, :],
                                     m0[0:SC, c:c + 1, :].to_broadcast([SC, 4, P]), start=False, stop=True,
                                     skip_group_check=True)
                    if r % 2 == 1:
                        last.then_inc(s[f"A{c}_sub"], 1)

            def per_head(bank, v_of, cc, e_of, query, n):
                for par in range(2):
                    for r in range(4):
                        last = pe.matmul(W[bank][32 * r:32 * r + 32, cc * S + query:cc * S + query + n],
                                         v_of(4 * cc + r, par), e_of(r, par), start=par == 0, stop=par == 1)
                return last

            with nc.tensor.Fori(2, last_t + 2) as t:
                pe.wait_ge(s["ld_ctx_A"], 16 * (t - 1))
                pe.wait_ge(s["T_lo_D"], t - 1)
                for oc in range(KC):
                    for kc in range(KC):
                        pe.matmul(W[2][:, oc * P:(oc + 1) * P], wc_of("k0", kc * D + oc * P, P), ctx_f["A"][:, kc, :],
                                  start=kc == 0, stop=False)
                    last = pe.matmul(W[2][:, oc * P:(oc + 1) * P], bias_row[:, oc * P:(oc + 1) * P], ones_row[:, :],
                                     start=False, stop=True)
                last.then_inc(s["k0_mm"], 1)
                pe.wait_ge(s["ln_C"], t - 1)
                transposes("C", 3)
                scores1(1, "T0", t - 1)
                pe.wait_ge(s["res_D"], t - 1)
                for cc in range(KC):
                    pe.wait_ge(s[f"T{cc}_exp"], half(1, t + (cc - 1)))
                    for bank, v, name in ((1, ones_pad, "zC_mm"), (0, v1_pad, "yC_mm")):
                        last = per_head(bank, lambda g, par: v[0:SC, 32 * par:32 * par + 32], cc,
                                        lambda r, par: e1[0:SC, cc, r, par, :], 0, S)
                        if cc == KC - 1:
                            last.then_inc(s[name], 1)
                pe.wait_ge(s["ln_A"], t)
                pe.wait_ge(s["zC"], t)
                transposes("A", 1)
                pe.wait_ge(s["T_lo_C"], t)
                queries("C", 3, "q1", False)
                pe.wait_ge(s["A1_p"], t)
                pe.wait_ge(s["k0_rest"], t)
                for c in range(NT):
                    for cc in range(KC):
                        last = per_head(2, lambda g, par: v0_pad[0:SC, g, 32 * par:32 * par + 32], cc,
                                        lambda r, par: e0[0:SC, c, r, 2 * cc + par, :], c * P, P)
                last.then_inc(s["yA_mm"], 1)
                pe.wait_ge(s["ld_ctx_C"], 16 * (t - 1))
                pe.wait_ge(s["q_rest_C"], t)
                for kc in range(KC):
                    pe.matmul(W[3][:, 0:P], wc_of("k1", kc * P, P), ctx_f["C"][:, kc, :],
                              start=kc == 0, stop=kc == KC - 1)
                for kc in range(KC):
                    last = pe.matmul(W[3][:, P:P + HD], ctx_f["C"][:, kc, :], wc_of("v1", kc * HD, HD),
                                     start=kc == 0, stop=kc == KC - 1)
                last.then_inc(s["kv1_mm"], 1)
                pe.wait_ge(s["yA_lo"], t)
                rows_out(2, y_hi["A"], y_lo["A"], "wo0", KC, True).then_inc(s["woA_mm"], 1)
                pe.wait_ge(s["T_lo_A"], t)
                queries("A", 1, "q0", True)
                pe.wait_ge(s["res_A"], t)
                for kc in range(KC):
                    pe.matmul(W[2][:, 0:D], ctx_f["A"][:, kc, :], wc_of("v0", kc * D, D), start=kc == 0, stop=False)
                pe.matmul(W[2][:, 0:D], ones_row[:, :], bias_row[:, D:2 * D], start=False, stop=True)\
                    .then_inc(s["v0_mm"], 1)
                pe.wait_ge(s["yC_lo"], t)
                rows_out(0, y_hi["C"], y_lo["C"], "wo1", KC).then_inc(s["woC_mm"], 1)
                pe.wait_ge(s["ln_B"], t)
                pe.wait_ge(s["v0_pad"], t)
                transposes("B", 2)
                pe.wait_ge(s["ld_q_C"], 16 * SLOTS * t)
                pe.wait_ge(s["ks1"], t)
                key_scores(0)
                pe.wait_ge(s["T_lo_B"], t)
                gate_up(0, 3, t)
                gate_up(1, 2, t)
                pe.wait_ge(s["M0_max"], t)
                key_scores(1)
                pe.wait_ge(s["q_rest_A"], t)
                gate_up(2, 1, t)
                pe.wait_ge(s["ln_D"], t)
                pe.wait_ge(s["G_h"], chunk(1, t))
                transposes("D", 2)
                gate_up(3, 3, t)
                pe.wait_ge(s["M1_max"], t)
                for c in range(NT):
                    last = pe.transpose(W[0][0:H, c * P:(c + 1) * P], m1[:, c, :], ident[:, :])
                last.then_inc(s["mT_mm"], 1)
                pe.wait_ge(s["ld_q_A"], 16 * SLOTS * t)
                pe.wait_ge(s["ld_k0"], 16 * SLOTS * t)
                scores0(0, t)
                pe.wait_ge(s["G_h"], chunk(2, t))
                gate_up(4, 1, t)
                pe.wait_ge(s["G_h"], chunk(3, t))
                gate_up(5, 3, t)
                subtract_max(0, t)
                pe.wait_ge(s["m_p2"], t)
                pe.wait_ge(s["T_lo_D"], t)
                rows_out(0, xt_hi["D"], xt_lo["D"], "f1", KC, True).then_inc(s["f1_mm"], 1)
                scores0(1, t)
                pe.wait_ge(s["G_lo"], chunk_lo(HC_POOL - 1, t))
                pe.wait_ge(s["G_lo_last"], t)
                rows_out(1, h_hi, h_lo, "down", HC).then_inc(s["dn_mm"], 1)
                subtract_max(1, t)
                pe.wait_ge(s["ld_m"], 16 * MAX_PARTS * t)
                scores1(0, "A1", t)

def kernel(**inputs):
    import concourse.bacc as bacc
    from concourse.bass_utils import run_bass_kernel_spmd

    a = {k: np.asarray(v) for k, v in inputs.items()}
    x, c = a["x"], a["ctx_1024"]
    batches = x.shape[0]
    T = batches + STAGES_BEHIND
    f = x.dtype

    def chunks(m):
        return m.reshape(-1, P, m.shape[1]).transpose(1, 0, 2).reshape(P, -1)

    perm = np.arange(D).reshape(HD, H).T.reshape(-1)
    perm_s1 = np.arange(D).reshape(KC, GP, HD).transpose(0, 2, 1).reshape(-1)
    perm_s = perm[perm_s1]
    xp = np.concatenate([np.zeros((FRONT_X, S, D), f), x, np.zeros((T + 1 - batches, S, D), f)])
    ct = c.transpose(0, 2, 1).reshape(batches, KC, P, SC).transpose(0, 2, 1, 3)
    cpad = np.zeros((FRONT_C + T + 1, P, KC, P), f)
    cpad[FRONT_C:FRONT_C + batches, :, :, :SC] = ct
    wc = np.concatenate([
        chunks(a["L0_xattn_Wk_w"].T[:, perm_s]), chunks(a["L0_xattn_Wv_w"].T[:, perm]),
        chunks(np.tile(a["L1_xattn_Wkv"][:, :HD], (1, P // HD))), chunks(a["L1_xattn_Wkv"][:, HD:])], axis=1)
    wf = np.concatenate([
        chunks(a["L0_xattn_Wq_w"].T[:, perm_s]), chunks(a["L1_xattn_Wq"][:, perm_s1]),
        chunks(a["L0_xattn_Wo_w"].T[perm]), chunks(a["L1_xattn_Wo"]), chunks(a["L1_ffn_W"].T)], axis=1)
    wi = np.concatenate([chunks(a["L0_ffn_w_gate"].T), chunks(a["L0_ffn_w_up"].T), chunks(a["L0_ffn_w_down"].T)], axis=1)
    brow = np.concatenate([a["L0_xattn_Wq_b"][perm_s], a["L0_xattn_Wk_b"][perm_s], a["L0_xattn_Wv_b"][perm],
                           a["L0_xattn_Wo_b"], a["L1_ffn_b"]])[None]
    gates = np.tile(np.concatenate([a["g_xattn"], a["g_ffn"]])[None], (P, 1))
    slot = np.arange(P) // HD
    off = [np.array([-1.0 if i < SLOTS and SLOT_K[i] > n else 0.0 for i in slot], f)[:, None] for n in (0, 1)]
    ones_pad = np.zeros((P, 64), f)
    ones_pad[:, 0:HD] = 1.0
    ones_pad[:, 48:48 + HD] = 1.0
    cst = np.concatenate([np.eye(P, dtype=f)] + off + [ones_pad], axis=1)
    arrays = {"xp": xp, "cp": cpad, "wc": wc, "wf": wf, "wi": wi, "brow": brow, "gates": gates, "cst": cst,
              "ldT": a["L1_ffn_lora_down"].T, "da": a["L1_ffn_down_aux"], "luT": a["L1_ffn_lora_up"].T,
              "uaT": a["L1_ffn_up_aux"].T}
    arrays = {k: np.ascontiguousarray(v) for k, v in arrays.items()}
    nc = bacc.Bacc("TRN2", target_bir_lowering=False, num_devices=1)
    aps = [nc.dram_tensor(k, v.shape, mybir.dt.from_np(v.dtype), kind="ExternalInput").ap() for k, v in arrays.items()]
    aps.append(nc.dram_tensor("y", (T, S, D), F32, kind="ExternalOutput").ap())
    flamingo_kernel(nc, *aps)
    r = run_bass_kernel_spmd(nc, [arrays], core_ids=[0])
    return r.results[0]["y"][STAGES_BEHIND:]
```
